# Optimizing a Trainium2 kernel written in Bass

```python
import numpy as np
import jax
import jax.numpy as jnp

def _softmax(x, axis=-1):
    return jax.nn.softmax(x, axis=axis)

def _gelu(x):
    return jax.nn.gelu(x, approximate=True)

def _silu(x):
    return jax.nn.silu(x)

def _sigmoid(x):
    return jax.nn.sigmoid(x)

def _layernorm(x, axis=-1, eps=1e-05):
    m = jnp.mean(x, axis=axis, keepdims=True)
    v = jnp.var(x, axis=axis, keepdims=True)
    return (x - m) / jnp.sqrt(v + eps)

def _scatter_add(tgt, idx, src, axis=0):
    return tgt.at[idx].add(src)

def _segment_sum(src, seg, n):
    return jax.ops.segment_sum(src, seg, n)
kernel_name = 'mk_hybrid_d1_jaxref_r4_1fb269'

def setup_inputs(seed: int=0):
    np.random.seed(seed)
    _w = jnp.asarray

    def _L0_attn_a_setup():
        import jax, jax.numpy as jnp
        import numpy as np
        import math
        D_MODEL, N_HEADS, RANK = (256, 16, 16)
        D_K = D_MODEL // N_HEADS
        BATCH, N = (2, 512)
        key = jax.random.key(seed)
        ks = jax.random.split(key, 8)
        s = 1.0 / math.sqrt(D_MODEL)
        sr = 1.0 / math.sqrt(D_K)
        return {'x': jax.random.normal(ks[0], (BATCH, N, D_MODEL), jnp.float32), 'WQ': jax.random.normal(ks[1], (D_MODEL, D_MODEL), jnp.float32) * s, 'bQ': jnp.zeros((D_MODEL,), jnp.float32), 'WK': jax.random.normal(ks[2], (D_MODEL, D_MODEL), jnp.float32) * s, 'bK': jnp.zeros((D_MODEL,), jnp.float32), 'WV': jax.random.normal(ks[3], (D_MODEL, D_MODEL), jnp.float32) * s, 'bV': jnp.zeros((D_MODEL,), jnp.float32), 'WO': jax.random.normal(ks[4], (D_MODEL, D_MODEL), jnp.float32) * s, 'bO': jnp.zeros((D_MODEL,), jnp.float32), 'WQr': jax.random.normal(ks[5], (D_K, RANK), jnp.float32) * sr, 'WKr': jax.random.normal(ks[6], (D_K, RANK), jnp.float32) * sr}
    _L0_attn_a_in = _L0_attn_a_setup()

    def _L0_attn_b_setup():
        import jax, jax.numpy as jnp
        import numpy as np
        from jax import lax
        B, L, D, N, DT_RANK = (2, 512, 256, 16, 64)

        def _assoc_op(left, right):
            a_l, b_l = left
            a_r, b_r = right
            return (a_r * a_l, a_r * b_l + b_r)
        key = jax.random.key(seed)
        ks = jax.random.split(key, 6)
        x = jax.random.normal(ks[0], (B, L, D), dtype=jnp.float32)
        A_log = jnp.log(jnp.broadcast_to(jnp.arange(1, N + 1, dtype=jnp.float32), (D, N)))
        D_param = jnp.ones((D,), dtype=jnp.float32)
        W_bc = jax.random.normal(ks[1], (D, 2 * N), dtype=jnp.float32) / np.sqrt(D)
        W_dt = jax.random.normal(ks[2], (D, DT_RANK), dtype=jnp.float32) / np.sqrt(D)
        W_dtproj = jax.random.normal(ks[3], (DT_RANK, D), dtype=jnp.float32) / np.sqrt(DT_RANK)
        dt = jax.random.uniform(ks[4], (D,), minval=0.001, maxval=0.1, dtype=jnp.float32)
        b_dtproj = dt + jnp.log(-jnp.expm1(-dt))
        return {'x': x, 'A_log': A_log, 'D_param': D_param, 'W_bc': W_bc, 'W_dt': W_dt, 'W_dtproj': W_dtproj, 'b_dtproj': b_dtproj}
    _L0_attn_b_in = _L0_attn_b_setup()

    def _L0_ffn_setup():
        import jax, jax.numpy as jnp
        import numpy as np
        B, S, D = (1, 512, 256)
        E, K, F = (64, 8, 192)
        SF = 192
        C = 128
        ROUTED_SCALE = 1.0

        def _moe_forward(x, router_w, w_gate, w_up, w_down, ws_gate_up, ws_down):
            T = x.shape[0]
            logits = x.astype(jnp.float32) @ router_w.T
            probs = jax.nn.softmax(logits, axis=-1)
            topk_w, topk_ids = jax.lax.top_k(probs, K)
            topk_w = topk_w / jnp.sum(topk_w, axis=-1, keepdims=True)
            topk_w = topk_w.astype(x.dtype)
            N = T * K
            flat_e = topk_ids.reshape(-1)
            flat_w = topk_w.reshape(-1)
            tok = jnp.arange(N) // K
            onehot = flat_e[:, None] == jnp.arange(E)[None, :]
            pos = jnp.cumsum(onehot, axis=0)[jnp.arange(N), flat_e] - 1
            valid = pos < C
            idx = jnp.where(valid, flat_e * C + pos, E * C)
            x_buf = jnp.zeros((E * C + 1, x.shape[1]), x.dtype).at[idx].set(x[tok])
            xb = x_buf[:E * C].reshape(E, C, -1)
            g = jnp.einsum('ecd,edf->ecf', xb, w_gate)
            u = jnp.einsum('ecd,edf->ecf', xb, w_up)
            h = jax.nn.silu(g) * u
            y = jnp.einsum('ecf,efd->ecd', h, w_down).reshape(E * C, -1)
            safe = jnp.where(valid, idx, 0)
            contrib = y[safe] * (flat_w * valid.astype(flat_w.dtype))[:, None]
            routed = jax.ops.segment_sum(contrib, tok, num_segments=T)
            routed = routed * ROUTED_SCALE
            gu = x @ ws_gate_up
            sg, su = (gu[:, :SF], gu[:, SF:])
            shared = jax.nn.silu(sg) * su @ ws_down
            return routed + shared
        key = jax.random.key(seed)
        ks = jax.random.split(key, 7)
        w = 0.02
        return {'hidden_states': jax.random.normal(ks[0], (B, S, D), jnp.float32), 'router_w': jax.random.normal(ks[1], (E, D), jnp.float32) * w, 'w_gate': jax.random.normal(ks[2], (E, D, F), jnp.float32) * w, 'w_up': jax.random.normal(ks[3], (E, D, F), jnp.float32) * w, 'w_down': jax.random.normal(ks[4], (E, F, D), jnp.float32) * w, 'ws_gate_up': jax.random.normal(ks[5], (D, 2 * SF), jnp.float32) * w, 'ws_down': jax.random.normal(ks[6], (SF, D), jnp.float32) * w}
    _L0_ffn_in = _L0_ffn_setup()
    _d = {'L0_attn_a_x': _L0_attn_a_in['x'], 'L0_attn_a_WQ': _L0_attn_a_in['WQ'], 'L0_attn_a_bQ': _L0_attn_a_in['bQ'], 'L0_attn_a_WK': _L0_attn_a_in['WK'], 'L0_attn_a_bK': _L0_attn_a_in['bK'], 'L0_attn_a_WV': _L0_attn_a_in['WV'], 'L0_attn_a_bV': _L0_attn_a_in['bV'], 'L0_attn_a_WO': _L0_attn_a_in['WO'], 'L0_attn_a_bO': _L0_attn_a_in['bO'], 'L0_attn_a_WQr': _L0_attn_a_in['WQr'], 'L0_attn_a_WKr': _L0_attn_a_in['WKr'], 'L0_attn_b_A_log': _L0_attn_b_in['A_log'], 'L0_attn_b_D_param': _L0_attn_b_in['D_param'], 'L0_attn_b_W_bc': _L0_attn_b_in['W_bc'], 'L0_attn_b_W_dt': _L0_attn_b_in['W_dt'], 'L0_attn_b_W_dtproj': _L0_attn_b_in['W_dtproj'], 'L0_attn_b_b_dtproj': _L0_attn_b_in['b_dtproj'], 'L0_ffn_router_w': _L0_ffn_in['router_w'], 'L0_ffn_w_gate': _L0_ffn_in['w_gate'], 'L0_ffn_w_up': _L0_ffn_in['w_up'], 'L0_ffn_w_down': _L0_ffn_in['w_down'], 'L0_ffn_ws_gate_up': _L0_ffn_in['ws_gate_up'], 'L0_ffn_ws_down': _L0_ffn_in['ws_down']}
    _x0 = _d['L0_attn_a_x']
    _d['L0_attn_a_x'] = jax.random.normal(jax.random.fold_in(jax.random.key(seed), 1), (2, 2048, 256), dtype=_x0.dtype)
    del _x0
    return _d

def reference(L0_attn_a_x, L0_attn_a_WQ, L0_attn_a_bQ, L0_attn_a_WK, L0_attn_a_bK, L0_attn_a_WV, L0_attn_a_bV, L0_attn_a_WO, L0_attn_a_bO, L0_attn_a_WQr, L0_attn_a_WKr, L0_attn_b_A_log, L0_attn_b_D_param, L0_attn_b_W_bc, L0_attn_b_W_dt, L0_attn_b_W_dtproj, L0_attn_b_b_dtproj, L0_ffn_router_w, L0_ffn_w_gate, L0_ffn_w_up, L0_ffn_w_down, L0_ffn_ws_gate_up, L0_ffn_ws_down):

    def _L0_attn_a_ref(x, WQ, bQ, WK, bK, WV, bV, WO, bO, WQr, WKr):
        import jax, jax.numpy as jnp
        import numpy as np
        import math
        D_MODEL, N_HEADS, RANK = (256, 16, 16)
        D_K = D_MODEL // N_HEADS
        BATCH, N = (2, 512)
        b, n, d = x.shape
        Q = (x @ WQ + bQ).reshape(b, n, N_HEADS, D_K)
        K = (x @ WK + bK).reshape(b, n, N_HEADS, D_K)
        V = (x @ WV + bV).reshape(b, n, N_HEADS, D_K)
        Qr = jnp.einsum('bnhd,dr->bnhr', Q, WQr)
        Kr = jnp.einsum('bnhd,dr->bnhr', K, WKr)
        scores = jnp.einsum('bnhr,bmhr->bnhm', Qr, Kr) / math.sqrt(RANK)
        A = jax.nn.softmax(scores, axis=-1)
        out = jnp.einsum('bnhm,bmhv->bnhv', A, V).reshape(b, n, d)
        return out @ WO + bO

    def _L0_attn_b_ref(x, A_log, D_param, W_bc, W_dt, W_dtproj, b_dtproj):
        import jax, jax.numpy as jnp
        import numpy as np
        from jax import lax
        B, L, D, N, DT_RANK = (2, 512, 256, 16, 64)

        def _assoc_op(left, right):
            a_l, b_l = left
            a_r, b_r = right
            return (a_r * a_l, a_r * b_l + b_r)
        x_bc = jnp.einsum('bld,dn->bln', x, W_bc)
        n = A_log.shape[1]
        B_sel = x_bc[..., :n]
        C_sel = x_bc[..., n:]
        dt_low = jnp.einsum('bld,dr->blr', x, W_dt)
        delta = jax.nn.softplus(jnp.einsum('blr,rd->bld', dt_low, W_dtproj) + b_dtproj)
        A = -jnp.exp(A_log)
        A_bar = jnp.exp(delta[..., None] * A)
        Bx = (delta * x)[..., None] * B_sel[:, :, None, :]
        _, all_h = lax.associative_scan(_assoc_op, (A_bar, Bx), axis=1)
        y = jnp.sum(C_sel[:, :, None, :] * all_h, axis=-1)
        return y + D_param * x

    def _L0_ffn_ref(hidden_states, router_w, w_gate, w_up, w_down, ws_gate_up, ws_down):
        import jax, jax.numpy as jnp
        import numpy as np
        B, S, D = (1, 512, 256)
        E, K, F = (64, 8, 192)
        SF = 192
        C = 128
        ROUTED_SCALE = 1.0

        def _moe_forward(x, router_w, w_gate, w_up, w_down, ws_gate_up, ws_down):
            T = x.shape[0]
            logits = x.astype(jnp.float32) @ router_w.T
            probs = jax.nn.softmax(logits, axis=-1)
            topk_w, topk_ids = jax.lax.top_k(probs, K)
            topk_w = topk_w / jnp.sum(topk_w, axis=-1, keepdims=True)
            topk_w = topk_w.astype(x.dtype)
            N = T * K
            flat_e = topk_ids.reshape(-1)
            flat_w = topk_w.reshape(-1)
            tok = jnp.arange(N) // K
            onehot = flat_e[:, None] == jnp.arange(E)[None, :]
            pos = jnp.cumsum(onehot, axis=0)[jnp.arange(N), flat_e] - 1
            valid = pos < C
            idx = jnp.where(valid, flat_e * C + pos, E * C)
            x_buf = jnp.zeros((E * C + 1, x.shape[1]), x.dtype).at[idx].set(x[tok])
            xb = x_buf[:E * C].reshape(E, C, -1)
            g = jnp.einsum('ecd,edf->ecf', xb, w_gate)
            u = jnp.einsum('ecd,edf->ecf', xb, w_up)
            h = jax.nn.silu(g) * u
            y = jnp.einsum('ecf,efd->ecd', h, w_down).reshape(E * C, -1)
            safe = jnp.where(valid, idx, 0)
            contrib = y[safe] * (flat_w * valid.astype(flat_w.dtype))[:, None]
            routed = jax.ops.segment_sum(contrib, tok, num_segments=T)
            routed = routed * ROUTED_SCALE
            gu = x @ ws_gate_up
            sg, su = (gu[:, :SF], gu[:, SF:])
            shared = jax.nn.silu(sg) * su @ ws_down
            return routed + shared
        b, s, d = hidden_states.shape
        x = hidden_states.reshape(-1, d)
        out = _moe_forward(x, router_w, w_gate, w_up, w_down, ws_gate_up, ws_down)
        return out.reshape(b, s, d)
    x = L0_attn_a_x
    x = x + _L0_attn_a_ref(_layernorm(x, axis=-1), L0_attn_a_WQ, L0_attn_a_bQ, L0_attn_a_WK, L0_attn_a_bK, L0_attn_a_WV, L0_attn_a_bV, L0_attn_a_WO, L0_attn_a_bO, L0_attn_a_WQr, L0_attn_a_WKr)
    x = x + _L0_ffn_ref(_layernorm(x, axis=-1), L0_ffn_router_w, L0_ffn_w_gate, L0_ffn_w_up, L0_ffn_w_down, L0_ffn_ws_gate_up, L0_ffn_ws_down)
    x = x + _L0_attn_b_ref(_layernorm(x, axis=-1), L0_attn_b_A_log, L0_attn_b_D_param, L0_attn_b_W_bc, L0_attn_b_W_dt, L0_attn_b_W_dtproj, L0_attn_b_b_dtproj)
    x = x + _L0_ffn_ref(_layernorm(x, axis=-1), L0_ffn_router_w, L0_ffn_w_gate, L0_ffn_w_up, L0_ffn_w_down, L0_ffn_ws_gate_up, L0_ffn_ws_down)
    return x

_drawn_inputs = setup_inputs


def setup_inputs(seed=0):
    import zlib

    import numpy as np

    out = dict(_drawn_inputs(seed))
    spreads = {'L0_attn_a_bQ': (0.0, 0.781),
     'L0_attn_a_bK': (0.0, 2.0),
     'L0_attn_a_bV': (0.0, 0.1),
     'L0_attn_a_bO': (0.0, 0.1),
     'L0_attn_b_D_param': (1.0, 0.2)}
    factors = {'L0_ffn_router_w': 8.0,
     'L0_ffn_w_gate': 8.0,
     'L0_ffn_w_up': 8.0,
     'L0_ffn_w_down': 8.0,
     'L0_ffn_ws_down': 2.9}
    for name, (base, spread) in spreads.items():
        noise = np.random.default_rng([zlib.crc32(name.encode()), seed]).standard_normal(out[name].shape)
        drawn = base * np.exp(spread * noise) if base else spread * noise
        out[name] = jnp.asarray(drawn.astype(out[name].dtype))
    for name, factor in factors.items():
        out[name] = (out[name] * factor).astype(out[name].dtype)
    return out
```

```python
from contextlib import ExitStack

import numpy as np

import concourse.bass as bass
from concourse import mybir

F32 = mybir.dt.float32
BF16 = mybir.dt.bfloat16
I32 = mybir.dt.int32
U32 = mybir.dt.uint32
ALU = mybir.AluOpType
ACT = mybir.ActivationFunctionType
AX = mybir.AxisListType

P = 128
BATCH, SEQ, D = 2, 2048, 256
TOK = BATCH * SEQ
TILES = TOK // P
DC = D // P
HEADS, DK = 16, 16
GT = 4
GROUP = GT * P
GROUPS = TOK // GROUP
KT = SEQ // P
QC = SEQ // GROUP
LN_EPS = 1e-5
BANK = 512
EXPERTS, TOP, CAP, FF = 64, 8, 128, 192
FC, FP = 2, 96
ROW = D + EXPERTS
NEG = -3.0e38
SPARE = TOK

Q_PARTS = (0, 1, 2, 0, 1, 0)
K_PARTS = (0, 0, 0, 1, 1, 2)
PAIR_ROWS = DK * len(Q_PARTS)
SHIFT_ROWS = 2
ROWS = PAIR_ROWS + SHIFT_ROWS


class Mem:

    def __init__(self, nc, ctx, tag):
        self.nc, self.ctx, self.tag = nc, ctx, tag
        self.sems = []
        ctx.callback(self.clear)

    def sb(self, name, shape, dt=F32):
        return self.ctx.enter_context(self.nc.sbuf_tensor(f"{self.tag}_{name}", shape, dt))

    def ps(self, name, shape, dt=F32):
        return self.ctx.enter_context(self.nc.psum_tensor(f"{self.tag}_{name}", shape, dt))

    def sem(self, name):
        self.sems.append(self.nc.alloc_semaphore(f"{self.tag}_{name}"))
        return self.sems[-1]

    def clear(self):
        if self.sems:
            self.nc.clear_and_free_semaphores(self.sems)
            self.nc.all_engine_barrier()


class Chain:

    def __init__(self, eng, sem, start=0):
        self.eng, self.sem, self.start, self.n = eng, sem, start, 0

    def __call__(self, ins):
        self.n += 1
        return ins.then_inc(self.sem, 1)

    def settle(self):
        self.eng.wait_ge(self.sem, v(self.start + self.n))


class Step:

    def __init__(self, eng, turn, a=1, b=0, held=None):
        self.eng, self.turn, self.a, self.b = eng, turn, a, b
        self.held = {} if held is None else held

    def __mul__(self, k):
        return Step(self.eng, self.turn, self.a * k, self.b * k, self.held)

    def __add__(self, k):
        return Step(self.eng, self.turn, self.a, self.b + k, self.held)

    def __sub__(self, k):
        return self + -k

    __rmul__, __radd__ = __mul__, __add__

    def value(self):
        if self.a not in self.held:
            self.held[self.a] = self.eng.snap(self.turn * self.a)
        return self.held[self.a] + self.b


def v(x):
    return x.value() if isinstance(x, Step) else x


def early(n, k):
    return isinstance(n, int) and n < k


def turns(eng, body, count, ring, first, last):
    assert (last - first) % ring == 0 and first >= 1
    for n in range(first):
        body(n, n % ring, n // ring, count - 1 - n)
    with eng.Fori(0, (last - first) // ring) as i:
        at = Step(eng, i)
        for n in range(first, first + ring):
            body(at * ring + n, n % ring, at + n // ring, count - last)
    for n in range(last, count):
        body(n, n % ring, n // ring, count - 1 - n)


def tile_of(x_sb, t):
    return x_sb[:, bass.ds(t, 1), :].rearrange("p a d -> p (a d)")


def make_identity(eng, tile, done, value):
    eng.memset(tile, 0.0).then_inc(done, 1)
    eng.wait_ge(done, value + 1)
    n = tile.shape[1]
    eng.affine_select(out=tile, in_=tile, compare_op=ALU.not_equal, fill=1.0, base=0,
                      pattern=[[-1, n]], channel_multiplier=1).then_inc(done, 1)


def layer_norm_stats(dve, own, rows, stats, mom, var_ready):
    for j, x in enumerate(rows):
        own(dve.bn_stats(stats[:, j, :], x))
    own.settle()
    own(dve.tensor_tensor(mom[:, 0, :], stats[:, :, 1], stats[:, :, 4], ALU.add))
    own(dve.tensor_tensor(mom[:, 1, :], stats[:, :, 1], stats[:, :, 4], ALU.subtract))
    own(dve.tensor_tensor(mom[:, 2, :], stats[:, :, 2], stats[:, :, 5], ALU.add))
    own.settle()
    own(dve.tensor_tensor(mom[:, 3, :], mom[:, 1, :], mom[:, 1, :], ALU.mult))
    own(dve.tensor_scalar(mom[:, 4, :], mom[:, 0, :], 0.5, None, ALU.mult))
    own(dve.tensor_scalar(mom[:, 2, :], mom[:, 2, :], 1.0 / D, LN_EPS, ALU.mult, ALU.add))
    own.settle()
    dve.scalar_tensor_tensor(out=mom[:, 5, :], in0=mom[:, 3, :], scalar=0.25, in1=mom[:, 2, :],
                             op0=ALU.mult, op1=ALU.add).then_inc(var_ready, 1)


def row_bcast(v, n):
    return v.rearrange("(a n) -> a n", a=1).to_broadcast([P, n])


def phase_qkv(nc, io, x_sb, v_sb, ident, q_dram, k_dram, sums, table):
    with ExitStack() as ctx:
        m = Mem(nc, ctx, "qkv")
        w_sb = {s: m.sb(f"w{s}", [P, DC, D]) for s in "qkv"}
        wT = m.sb("wT", [P, DC, D])
        wr = {s: m.sb(f"wr{s}", [P, P]) for s in "qk"}
        wf = {s: m.sb(f"wf{s}", [P, DC, D]) for s in "qk"}
        bcol = {s: m.sb(f"bcol{s}", [P, DC]) for s in "qk"}
        bf = m.sb("bf", [P, 2, DC])
        bv = m.sb("bv", [P, D])
        stats = m.sb("stats", [P, GT, 6])
        mom = m.sb("mom", [P, 6, GT])
        mhalf = m.sb("mhalf", [P, GT])
        rstd = m.sb("rstd", [P, GT])
        xn = m.sb("xn", [P, GT, D])
        xnT = m.sb("xnT", [P, DC, GROUP])
        full = m.sb("full", [P, 2, GROUP])
        rest = m.sb("rest", [P, 2, GROUP])
        parts = m.sb("parts", [P, 4, 3, GROUP], BF16)
        zeros = m.sb("zeros", [P, ROW])

        pT = m.ps("pT", [P, DC, BANK])
        pQK = m.ps("pQK", [P, 4, BANK])
        pV = m.ps("pV", [P, 2, BANK])

        w_in = m.sem("w_in")
        x_in = m.sem("x_in")
        consts = m.sem("consts")
        cleared = m.sem("cleared")
        blocks = m.sem("blocks")
        wt_done = m.sem("wt_done")
        wt_out = m.sem("wt_out")
        wf_done = m.sem("wf_done")
        wf_out = m.sem("wf_out")
        dve_own = m.sem("dve_own")
        var_ready = m.sem("var_ready")
        rstd_ready = m.sem("rstd_ready")
        xn_ready = m.sem("xn_ready")
        turned = m.sem("turned")
        xnT_ready = m.sem("xnT_ready")
        qk_done = m.sem("qk_done")
        v_done = m.sem("v_done")
        v_out = m.sem("v_out")
        full_ready = m.sem("full_ready")
        part0_ready = m.sem("part0_ready")
        parts_ready = m.sem("parts_ready")
        stored = m.sem("stored")
        block = ctx.enter_context(nc.Block())

        weights = {"q": io["WQ"], "k": io["WK"], "v": io["WV"]}
        biases = {"q": io["bQ"], "k": io["bK"]}
        ranks = {"q": io["WQr"], "k": io["WKr"]}

        @block.sync
        def _(sp):
            xs = io["x"].rearrange("b (t p) d -> p (b t) d", p=P)
            for n in range(4):
                sp.dma_start(x_sb[:, 8 * n:8 * n + 8, :], xs[:, 8 * n:8 * n + 8, :]).then_inc(x_in, 16)
            with sp.Fori(0, GROUPS) as g:
                b, col = g // QC, (g % QC) * GROUP
                for j in range(4):
                    sp.wait_ge(parts_ready, 4 * g + j + 1)
                    side, c2 = (q_dram, k_dram)[j // 2], j % 2
                    dst = side.rearrange("a (b r) n -> r a b n", b=BATCH)
                    sp.dma_start(dst[c2 * P:(c2 + 1) * P, :, bass.ds(b, 1), bass.ds(col, GROUP)]
                                 .rearrange("r a b n -> r a (b n)"), parts[:, j, :, :]).then_inc(stored, 16)
            sp.wait_ge(stored, 16 * 4 * GROUPS)

        @block.gpsimd
        def _(pool):
            make_identity(pool, ident[:, :], consts, 0)
            pool.memset(mhalf[:, :], -0.5).then_inc(consts, 1)
            pool.memset(wr["q"][:, :], 0.0).then_inc(consts, 1)
            pool.memset(wr["k"][:, :], 0.0).then_inc(consts, 1)
            pool.memset(zeros[:, :], 0.0).then_inc(consts, 1)
            with pool.Fori(0, GROUPS) as g:
                pool.wait_ge(var_ready, g + 1)
                pool.tensor_tensor(rstd[:, :], mom[:, 5, :], mhalf[:, :], ALU.pow).then_inc(rstd_ready, 1)

        @block.scalar
        def _(act):
            for s in "qkv":
                act.dma_start(w_sb[s][:, :, :], weights[s].rearrange("(c p) n -> p c n", p=P)).then_inc(w_in, 16)
            act.dma_start(bv[:, :], row_bcast(io["bV"], D)).then_inc(w_in, 16)
            with nc.allow_non_contiguous_dma(reason="two bias columns"):
                for s in "qk":
                    act.dma_start(bcol[s][:, :], biases[s].rearrange("(c p) -> p c", p=P)).then_inc(w_in, 16)
            act.wait_ge(consts, 5)
            for s in "qk":
                for h in range(P // DK):
                    act.dma_start(wr[s][DK * h:DK * h + DK, DK * h:DK * h + DK], ranks[s]).then_inc(blocks, 16)
            act.wait_ge(consts, 6)
            for to in sums:
                act.dma_start(to.rearrange("(t p) c -> p t c", p=P),
                              zeros[:, 0:D].rearrange("p (a c) -> p a c", a=1).to_broadcast([P, TILES + 1, D]))\
                   .then_inc(cleared, 16)
            act.dma_start(table[SPARE:SPARE + P, :], zeros[:, :]).then_inc(cleared, 16)
            with act.Fori(0, GROUPS) as g:
                for c in range(DC):
                    act.wait_ge(turned, 2 * g + c + 1)
                    if c == 0:
                        act.wait_ge(v_done, GT * g)
                    act.activation(xnT[:, c, :], pT[:, c, :], ACT.Copy).then_inc(xnT_ready, 1)
                for j in range(4):
                    act.wait_ge(qk_done, 4 * g + j + 1)
                    act.wait_ge(parts_ready, 4 * g + max(j - 1, 0))
                    act.activation(full[:, j % 2, :], pQK[:, j, :], ACT.Identity,
                                   bias=bf[:, j // 2, j % 2:j % 2 + 1]).then_inc(full_ready, 1)
                    act.wait_ge(stored, 16 * (4 * g))
                    act.activation(parts[:, j, 0, :], pQK[:, j, :], ACT.Identity,
                                   bias=bf[:, j // 2, j % 2:j % 2 + 1]).then_inc(part0_ready, 1)
            act.wait_ge(cleared, 16 * (len(sums) + 1))

        @block.vector
        def _(dve):
            for n, s in enumerate("qk"):
                dve.wait_ge(wt_done, n + 1)
                if n:
                    dve.wait_ge(wf_done, n)
                for c in range(DC):
                    dve.tensor_copy(wT[:, c, :], pT[:, c, 0:D]).then_inc(wt_out, 1)
                dve.wait_ge(wf_done, n + 1)
                for c in range(DC):
                    dve.tensor_copy(wf[s][:, c, :], pQK[:, c, 0:D]).then_inc(wf_out, 1)
                dve.tensor_copy(bf[:, n, :], pQK[:, 2, 0:DC]).then_inc(wf_out, 1)
            dve.wait_ge(x_in, 64)
            dve.wait_ge(w_in, 96)
            dve.wait_ge(consts, 3)
            with dve.Fori(0, GROUPS) as g:
                own = Chain(dve, dve_own, g * 18)
                layer_norm_stats(dve, own, [x_sb[:, bass.ds(g * GT + j, 1), :].rearrange("p a d -> p (a d)")
                                            for j in range(GT)], stats, mom, var_ready)
                dve.wait_ge(rstd_ready, g + 1)
                dve.wait_ge(turned, 2 * g)
                for j in range(GT):
                    dve.tensor_scalar(xn[:, j, :], x_sb[:, bass.ds(g * GT + j, 1), :].rearrange("p a d -> p (a d)"),
                                      mom[:, 4, j:j + 1], rstd[:, j:j + 1],
                                      ALU.subtract, ALU.mult).then_inc(xn_ready, 1)
                for j in range(4):
                    dve.wait_ge(part0_ready, 4 * g + j + 1)
                    dve.wait_ge(full_ready, 4 * g + j + 1)
                    own(dve.tensor_tensor(rest[:, j % 2, :], full[:, j % 2, :], parts[:, j, 0, :], ALU.subtract))
                    own.settle()
                    own(dve.tensor_copy(parts[:, j, 1, :], rest[:, j % 2, :]))
                    own.settle()
                    dve.tensor_tensor(parts[:, j, 2, :], rest[:, j % 2, :], parts[:, j, 1, :],
                                      ALU.subtract).then_inc(parts_ready, 1)
                for j in range(GT):
                    dve.wait_ge(v_done, GT * g + j + 1)
                    b, kt = g // QC, (g % QC) * GT + j
                    dve.tensor_tensor(v_sb[:, bass.ds(b, 1), :, bass.ds(kt, 1), :].rearrange("p b h t d -> p (b h) (t d)"),
                                      pV[:, j % 2, 0:D].rearrange("p (h d) -> p h d", h=HEADS),
                                      bv[:, :].rearrange("p (h d) -> p h d", h=HEADS), ALU.add).then_inc(v_out, 1)
                assert own.n == 18

        @block.tensor
        def _(pe):
            pe.wait_ge(consts, 5)
            pe.wait_ge(w_in, 96)
            pe.wait_ge(blocks, 16 * 2 * (P // DK))
            for n, s in enumerate("qk"):
                if n:
                    pe.wait_ge(wt_out, 2 * n)
                for c2 in range(DC):
                    for c in range(DC):
                        t = pe.transpose(pT[:, c2, c * P:(c + 1) * P], w_sb[s][:, c, c2 * P:(c2 + 1) * P], ident[:, :])
                t.then_inc(wt_done, 1)
                pe.wait_ge(wt_out, 2 * (n + 1))
                if n:
                    pe.wait_ge(wf_out, 3 * n)
                for c in range(DC):
                    for c2 in range(DC):
                        pe.matmul(pQK[:, c, c2 * P:(c2 + 1) * P], wT[:, c2, c * P:(c + 1) * P], wr[s][:, :],
                                  start=True, stop=True)
                for c2 in range(DC):
                    t = pe.matmul(pQK[:, 2, c2:c2 + 1], wr[s][:, :], bcol[s][:, c2:c2 + 1], start=True, stop=True)
                t.then_inc(wf_done, 1)
            pe.wait_ge(wf_out, 6)
            with pe.Fori(0, GROUPS) as g:
                for c in range(DC):
                    for j in range(GT):
                        if c == 0:
                            pe.wait_ge(xn_ready, GT * g + j + 1)
                            if j == 0:
                                pe.wait_ge(xnT_ready, 2 * g)
                        t = pe.transpose(pT[:, c, j * P:(j + 1) * P], xn[:, j, c * P:(c + 1) * P], ident[:, :])
                    t.then_inc(turned, 1)
                pe.wait_ge(xnT_ready, 2 * g + 2)
                for j in range(4):
                    s, c2 = "qk"[j // 2], j % 2
                    pe.wait_ge(part0_ready, 4 * g)
                    pe.wait_ge(full_ready, 4 * g)
                    for c in range(DC):
                        t = pe.matmul(pQK[:, j, :], wf[s][:, c, c2 * P:(c2 + 1) * P], xnT[:, c, :],
                                      start=(c == 0), stop=(c == DC - 1))
                    t.then_inc(qk_done, 1)
                for j in range(GT):
                    pe.wait_ge(v_out, GT * g + max(j - 1, 0))
                    for c in range(DC):
                        t = pe.matmul(pV[:, j % 2, 0:D], xnT[:, c, j * P:(j + 1) * P], w_sb["v"][:, c, :],
                                      start=(c == 0), stop=(c == DC - 1))
                    t.then_inc(v_done, 1)


def phase_attention(nc, v_sb, a_sb, q_dram, k_dram):
    SLOTS = 3
    NH = BATCH * HEADS
    STEPS = QC * KT
    HALF = 8
    GR = STEPS // HALF
    LEAD = KT
    LOADS = 2 * len(Q_PARTS)
    FIRST, LAST = 1, NH - 4
    assert (LAST - FIRST) % SLOTS == 0 and STEPS % SLOTS == 1
    with ExitStack() as ctx:
        m = Mem(nc, ctx, "att")
        qs = [m.sb(f"qs{s}", [ROWS, SEQ], BF16) for s in range(SLOTS)]
        ks = [m.sb(f"ks{s}", [ROWS, SEQ], BF16) for s in range(SLOTS)]
        vh = [m.sb(f"vh{s}", [P, KT, DK + 1]) for s in range(SLOTS)]
        probs = m.sb("probs", [P, 2 * HALF, GROUP])
        mx4 = [m.sb(f"mx4{s}", [P, KT, QC]) for s in range(SLOTS)]
        mx = m.sb("mx", [P, KT])
        nm = m.sb("nm", [P, SHIFT_ROWS, KT], BF16)
        nmT = m.sb("nmT", [SHIFT_ROWS * KT, P], BF16)
        identb = m.sb("identb", [P, P], BF16)
        comb = m.sb("comb", [P, DK + 1])
        acc_sb = m.sb("acc_sb", [P, 2, GROUP])
        rden = m.sb("rden", [P, KT])

        pR = m.ps("pR", [P, 3, BANK])
        pS = m.ps("pS", [P, 3, BANK])
        pA = m.ps("pA", [P, BANK])
        pO = m.ps("pO", [P, BANK])
        O = pO[:, 0:KT * (DK + 1)].rearrange("p (t d) -> p t d", d=DK + 1)
        NT = pO[0:SHIFT_ROWS * KT, 384:384 + P]

        qk_in = [m.sem(f"qk_in{s}") for s in range(SLOTS)]
        shift_in = [m.sem(f"shift_in{s}") for s in range(SLOTS)]
        consts = m.sem("consts")
        acc_clear = m.sem("acc_clear")
        v_in = m.sem("v_in")
        row_scored = m.sem("row_scored")
        maxed = m.sem("maxed")
        col_scored = m.sem("col_scored")
        expd = m.sem("expd")
        summed = m.sem("summed")
        acc_out = m.sem("acc_out")
        combined = m.sem("combined")
        mx_ready = m.sem("mx_ready")
        nm_hi = m.sem("nm_hi")
        nm_ready = m.sem("nm_ready")
        nm_turned = m.sem("nm_turned")
        nmT_ready = m.sem("nmT_ready")
        inverted = m.sem("inverted")
        normed = m.sem("normed")
        block = ctx.enter_context(nc.Block())

        def heads(eng, head, first=FIRST, last=LAST):
            for n in range(first):
                head(n, n % SLOTS, n // SLOTS, NH - 1 - n)
            with eng.Fori(0, (last - first) // SLOTS) as i:
                at = Step(eng, i)
                for n in range(first, first + SLOTS):
                    head(SLOTS * at + n, n % SLOTS, at + n // SLOTS, SLOTS)
            for n in range(last, NH):
                head(n, n % SLOTS, n // SLOTS, NH - 1 - n)

        def start(n):
            return isinstance(n, int) and n == 0

        @block.sync
        def _(sp):
            def load(n, s):
                for side, tile, sel in ((q_dram, qs[s], Q_PARTS), (k_dram, ks[s], K_PARTS)):
                    for r, part in enumerate(sel):
                        sp.dma_start(tile[DK * r:DK * r + DK, :],
                                     side[part, bass.ds(v(n * DK), DK), :]).then_inc(qk_in[s], 16)

            def shift(n, s):
                sp.wait_ge(nmT_ready, v(n + 1))
                for r in range(SHIFT_ROWS):
                    sp.dma_start(qs[s][PAIR_ROWS + r:PAIR_ROWS + r + 1, :].rearrange("a (t n) -> a t n", t=KT),
                                 nmT[KT * r:KT * r + KT, :]).then_inc(shift_in[s], 16)

            def head(n, s, turn, ahead):
                if ahead >= 2:
                    if not start(n):
                        sp.wait_ge(summed, v(GR * n - 1))
                    load(n + 2, (s + 2) % SLOTS)
                if ahead >= 1:
                    shift(n + 1, (s + 1) % SLOTS)

            load(0, 0)
            load(1, 1)
            shift(0, 0)
            heads(sp, head)

        @block.gpsimd
        def _(pool):
            make_identity(pool, identb[:, :], consts, 0)
            pool.memset(comb[:, :], 0.0).then_inc(consts, 1)
            for q in range(4):
                pool.wait_ge(consts, 3 + q)
                pool.affine_select(out=comb[:, :], in_=comb[:, :], compare_op=ALU.not_equal, fill=1.0,
                                   base=-32 * q, pattern=[[-1, DK + 1]], channel_multiplier=1).then_inc(consts, 1)
            for s in range(SLOTS):
                pool.wait_ge(consts, 7 + 2 * s)
                pool.memset(ks[s][PAIR_ROWS:ROWS, :], 1.0).then_inc(consts, 1)
                pool.wait_ge(consts, 8 + 2 * s)
                pool.memset(vh[s][:, :, DK:DK + 1], 1.0).then_inc(consts, 1)
            pool.wait_ge(consts, 7 + 2 * SLOTS)

            def fetch(n, s):
                src = v_sb[:, :, :, :, :].rearrange("p b h t d -> p (b h) t d")[:, bass.ds(v(n), 1), :, :]
                pool.tensor_copy(vh[s][:, :, 0:DK], src.rearrange("p n t d -> p (n t) d")).then_inc(v_in, 1)

            def head(n, s, turn, ahead):
                if ahead >= 2:
                    if not start(n):
                        pool.wait_ge(summed, v(GR * n))
                    fetch(n + 2, (s + 2) % SLOTS)

            fetch(0, 0)
            fetch(1, 1)
            heads(pool, head)

        @block.scalar
        def _(act):
            def drain(n, c, waits=True):
                act.wait_ge(summed, v(GR * n + 2 * c + 2))
                if waits:
                    act.wait_ge(combined, v(QC * n + c - 1))
                act.activation(acc_sb[:, c % 2, :], pA[:, :], ACT.Copy).then_inc(acc_out, 1)

            def head(n, s, turn, ahead):
                for g in range(GR):
                    if not (start(n) and g < 2):
                        act.wait_ge(summed, v(GR * n + g - 1))
                    for j in range(HALF):
                        k = HALF * g + j
                        if j == 1 and g % 2:
                            if g > 1:
                                drain(n, (g - 3) // 2, not (start(n) and g < 7))
                            elif not start(n):
                                drain(n - 1, QC - 1)
                        act.wait_ge(col_scored, v(STEPS * n + k + 1))
                        act.activation(probs[:, k % (2 * HALF), :], pS[:, (s + k) % 3, :], ACT.Exp,
                                       scale=float(DK) ** -0.5).then_inc(expd, 1)

            heads(act, head)
            drain(NH - 1, QC - 1)

        @block.vector
        def _(dve):
            dve.memset(pA[:, :], 0.0).then_inc(acc_clear, 1)

            def maxima(n, s, steps):
                for k in steps:
                    dve.wait_ge(row_scored, v(STEPS * n + k + 1))
                    dve.tensor_reduce(mx4[s][:, k // QC, k % QC:k % QC + 1], pR[:, (s + k) % 3, :],
                                      AX.X, ALU.max).then_inc(maxed, 1)

            def negate(n, s):
                dve.wait_ge(maxed, v(STEPS * n + STEPS))
                dve.tensor_reduce(mx[:, :], mx4[s][:, :, :], AX.X, ALU.max).then_inc(mx_ready, 1)
                dve.wait_ge(mx_ready, v(n + 1))
                dve.wait_ge(nm_turned, v(n))
                dve.tensor_scalar(nm[:, 0, :], mx[:, :], -1.0, None, ALU.mult).then_inc(nm_hi, 1)
                dve.wait_ge(nm_hi, v(n + 1))
                dve.scalar_tensor_tensor(out=nm[:, 1, :], in0=mx[:, :], scalar=-1.0, in1=nm[:, 0, :],
                                         op0=ALU.mult, op1=ALU.subtract).then_inc(nm_ready, 1)

            def send(n, s, turn_before, first=False):
                dve.wait_ge(nm_turned, v(n + 1))
                if not first:
                    dve.wait_ge(shift_in[(s + 2) % SLOTS], v(16 * SHIFT_ROWS * (turn_before + 1)))
                dve.tensor_copy(nmT[:, :], NT).then_inc(nmT_ready, 1)

            def normalise(n):
                dve.wait_ge(combined, v(QC * n + QC))
                dve.reciprocal(rden[:, :], O[:, :, DK:DK + 1].rearrange("p t a -> p (t a)")).then_inc(inverted, 1)
                dve.wait_ge(inverted, v(n + 1))
                dst = a_sb[:, :, :, :, :].rearrange("p b h t d -> p (b h) t d")[:, bass.ds(v(n), 1), :, :]
                dve.tensor_tensor(dst.rearrange("p n t d -> p (n t) d"), O[:, :, 0:DK],
                                  rden[:, :].rearrange("p (t a) -> p t a", a=1).to_broadcast([P, KT, DK]),
                                  ALU.mult).then_inc(normed, 1)

            def head(n, s, turn, ahead):
                s1, s2 = (s + 1) % SLOTS, (s + 2) % SLOTS
                if ahead >= 1:
                    maxima(n + 1, s1, range(LEAD, 2 * LEAD))
                if not start(n):
                    normalise(n - 1)
                if ahead >= 1:
                    maxima(n + 1, s1, range(2 * LEAD, STEPS))
                    negate(n + 1, s1)
                if ahead >= 2:
                    maxima(n + 2, s2, range(LEAD // 2))
                if ahead >= 1:
                    send(n + 1, s1, turn)
                if ahead >= 2:
                    maxima(n + 2, s2, range(LEAD // 2, LEAD))

            maxima(0, 0, range(STEPS))
            negate(0, 0)
            send(0, 0, 0, first=True)
            maxima(1, 1, range(LEAD))
            heads(dve, head)
            normalise(NH - 1)
            dve.wait_ge(normed, NH)

        @block.tensor
        def _(pe):
            pe.wait_ge(consts, 2 + 1 + 4 + 2 * SLOTS)
            pe.wait_ge(acc_clear, 1)

            def row_score(n, s, turn, k, first=False):
                if k == 0:
                    pe.wait_ge(qk_in[s], v(16 * LOADS * (turn + 1)))
                if not first:
                    pe.wait_ge(maxed, v(STEPS * n + k - 2))
                t, c = k // QC, k % QC
                pe.matmul(pR[:, (s + k) % 3, :], qs[s][0:PAIR_ROWS, t * P:(t + 1) * P],
                          ks[s][0:PAIR_ROWS, c * GROUP:(c + 1) * GROUP], start=True, stop=True).then_inc(row_scored, 1)

            def col_score(n, s, turn, k):
                if k == 0:
                    pe.wait_ge(shift_in[s], v(16 * SHIFT_ROWS * (turn + 1)))
                if not (start(n) and k < 3):
                    pe.wait_ge(expd, v(STEPS * n + k - 2))
                c, t = k // KT, k % KT
                pe.matmul(pS[:, (s + k) % 3, :], ks[s][:, t * P:(t + 1) * P],
                          qs[s][:, c * GROUP:(c + 1) * GROUP], start=True, stop=True).then_inc(col_scored, 1)

            def values(n, s, g, half):
                if half == 0:
                    pe.wait_ge(expd, v(STEPS * n + HALF * (g + 1)))
                    if g == 0:
                        pe.wait_ge(v_in, v(n + 1))
                    if g % 2 == 0:
                        pe.wait_ge(acc_out, v(QC * n + g // 2))
                for j in range(4 * half, 4 * half + 4):
                    t = (HALF * g + j) % KT
                    q = 32 * (j % 4)
                    mm = pe.matmul(pA[q:q + DK + 1, :], vh[s][:, t, :], probs[:, (HALF * g + j) % (2 * HALF), :],
                                   start=(t < 4), stop=(t >= KT - 4), skip_group_check=True)
                if half:
                    mm.then_inc(summed, 1)

            def combine(n, c, ahead):
                pe.wait_ge(acc_out, v(QC * n + c + 1))
                if c == 0 and not start(n):
                    pe.wait_ge(normed, v(n))
                if c == 2 and ahead:
                    pe.wait_ge(nmT_ready, v(n + 2))
                for t in range(GT):
                    mm = pe.matmul(O[:, c * GT + t, :], acc_sb[:, c % 2, t * P:(t + 1) * P], comb[:, :],
                                   start=True, stop=True)
                mm.then_inc(combined, 1)

            def turn_maxima(n, first=False):
                pe.wait_ge(nm_ready, v(n + 1))
                pe.wait_ge(nmT_ready, v(n))
                pe.matmul(NT, nm[:, :, :].rearrange("p r t -> p (r t)"), identb[:, :],
                          start=True, stop=True).then_inc(nm_turned, 1)

            def last_values(n, s, g, half):
                if g > 0:
                    values(n, s, g - 1, half)
                elif not start(n):
                    values(n - 1, (s + 2) % SLOTS, GR - 1, half)

            def head(n, s, turn, ahead):
                for g in range(GR):
                    for j in range(HALF):
                        k = HALF * g + j
                        col_score(n, s, turn, k)
                        over = (k + LEAD) // STEPS
                        if ahead >= 1 + over:
                            s_ahead = (s + 1 + over) % SLOTS
                            row_score(n + 1 + over, s_ahead, turn + (s + 1 + over) // SLOTS, (k + LEAD) % STEPS)
                        if j == 3:
                            last_values(n, s, g, 0)
                    if g % 2:
                        if g > 1:
                            combine(n, (g - 3) // 2, ahead)
                        elif not start(n):
                            combine(n - 1, QC - 1, 0)
                    last_values(n, s, g, 1)
                    if g == 6 and ahead >= 1:
                        turn_maxima(n + 1)

            for k in range(STEPS):
                row_score(0, 0, 0, k, first=(k < 3))
            turn_maxima(0)
            for k in range(LEAD):
                row_score(1, 1, 0, k)
            heads(pe, head)
            for half in range(2):
                values(NH - 1, (NH - 1) % SLOTS, GR - 1, half)
            combine(NH - 1, QC - 1, 0)


def phase_attention_out(nc, io, x_sb, a_sb, ident):
    with ExitStack() as ctx:
        m = Mem(nc, ctx, "wo")
        wo = m.sb("wo", [P, DC, D])
        bo = m.sb("bo", [P, D])
        rows = m.sb("rows", [P, GT, D])
        aT = m.sb("aT", [P, DC, GROUP])
        pT = m.ps("pT", [P, DC, BANK])
        pO = m.ps("pO", [P, 2, BANK])
        w_in = m.sem("w_in")
        staged = m.sem("staged")
        turned = m.sem("turned")
        aT_ready = m.sem("aT_ready")
        made = m.sem("made")
        biased = m.sem("biased")
        added = m.sem("added")
        block = ctx.enter_context(nc.Block())

        @block.sync
        def _(sp):
            sp.dma_start(wo[:, :, :], io["WO"].rearrange("(c p) n -> p c n", p=P)).then_inc(w_in, 16)
            sp.dma_start(bo[:, :], row_bcast(io["bO"], D)).then_inc(w_in, 16)

        @block.gpsimd
        def _(pool):
            pool.wait_ge(w_in, 32)
            with pool.Fori(0, GROUPS) as g:
                rows_g = x_sb[:, bass.ds(g * GT, GT), :]
                pool.tensor_tensor(rows_g, rows_g,
                                   bo[:, :].rearrange("p (a n) -> p a n", a=1).to_broadcast([P, GT, D]),
                                   ALU.add).then_inc(biased, 1)

        @block.scalar
        def _(act):
            def stage(n):
                if not early(n, 1):
                    act.wait_ge(turned, v(n))
                src = a_sb[:, bass.ds(v(n) // QC, 1), :, bass.ds((v(n) % QC) * GT, GT), :]
                act.activation(rows[:, :, :].rearrange("p t (h d) -> p h t d", d=DK),
                               src.rearrange("p b h t d -> p (b h) t d"), ACT.Copy).then_inc(staged, 1)

            def group(n, s, turn, ahead):
                act.wait_ge(turned, v(n + 1))
                if not early(n, 1):
                    act.wait_ge(made, v(n * 2))
                act.activation(aT[:, :, :], pT[:, :, :], ACT.Copy).then_inc(aT_ready, 1)
                if ahead:
                    stage(n + 1)
            stage(0)
            turns(act, group, GROUPS, 2, 2, GROUPS - 2)

        @block.vector
        def _(dve):
            def group(n, s, turn, ahead):
                for j in range(2):
                    dve.wait_ge(made, v(n * 2 + (j + 1)))
                    dve.wait_ge(biased, v(n + 1))
                    pair = x_sb[:, bass.ds(v(n * GT) + 2 * j, 2), :]
                    dve.tensor_tensor(pair, pair, pO[:, j, :].rearrange("p (t d) -> p t d", t=2), ALU.add)\
                       .then_inc(added, 1)
            turns(dve, group, GROUPS, 2, 2, GROUPS - 2)
            dve.wait_ge(added, 2 * GROUPS)

        @block.tensor
        def _(pe):
            pe.wait_ge(w_in, 32)

            def group(n, s, turn, ahead):
                pe.wait_ge(staged, v(n + 1))
                if not early(n, 1):
                    pe.wait_ge(aT_ready, v(n))
                for c in range(DC):
                    for t in range(GT):
                        mm = pe.transpose(pT[:, c, t * P:(t + 1) * P], rows[:, t, c * P:(c + 1) * P], ident[:, :])
                mm.then_inc(turned, 1)
                pe.wait_ge(aT_ready, v(n + 1))
                for j in range(2):
                    if not early(n, 1):
                        pe.wait_ge(added, v(n * 2 + (j - 1)))
                    for t in range(2):
                        for c in range(DC):
                            mm = pe.matmul(pO[:, j, t * D:(t + 1) * D], aT[:, c, (2 * j + t) * P:(2 * j + t + 1) * P],
                                           wo[:, c, :], start=(c == 0), stop=(c == DC - 1))
                    mm.then_inc(made, 1)
            turns(pe, group, GROUPS, 2, 2, GROUPS - 2)


def phase_route(nc, io, tag, x_sb, ident, table, order):
    G = 4
    N = TILES // G
    HT = TILES // 2
    with ExitStack() as ctx:
        m = Mem(nc, ctx, tag)
        rw = m.sb("rw", [EXPERTS, D])
        rwT = m.sb("rwT", [P, DC, EXPERTS])
        wgu = m.sb("wgu", [P, DC, 2 * FF])
        wd = m.sb("wd", [FP, FC, D])
        ranki = m.sb("ranki", [P, TILES], I32)
        rank = m.sb("rank", [P, TILES])
        stats = m.sb("stats", [P, G, 6])
        mom = m.sb("mom", [P, 6, G])
        mhalf = m.sb("mhalf", [P, G])
        rstd = m.sb("rstd", [P, G])
        rows = m.sb("rows", [P, 2, G, ROW])
        xnT = m.sb("xnT", [P, DC, GROUP])
        lg = m.sb("lg", [P, G, EXPERTS])
        less = m.sb("less", [P, G, EXPERTS])
        mx = m.sb("mx", [P, G])
        left = m.sb("left", [P, G, EXPERTS])
        top = m.sb("top", [P, G, TOP])
        mask = m.sb("mask", [P, G, EXPERTS])
        ex = m.sb("ex", [P, G, EXPERTS])
        exm = m.sb("exm", [P, G, EXPERTS])
        den = m.sb("den", [P, G])
        rden = m.sb("rden", [P, G])
        val = m.sb("val", [P, 2, 2, EXPERTS])
        sg = m.sb("sg", [FP, FC, GROUP])
        hh = m.sb("hh", [FP, FC, GROUP])

        pT = m.ps("pT", [P, DC, BANK])
        pG = m.ps("pG", [P, 2 * FC, BANK])
        pL = m.ps("pL", [P, BANK])
        pD = m.ps("pD", [P, BANK])
        LG = pL[:, 0:G * EXPERTS]
        VT = pL[:, G * EXPERTS:G * EXPERTS + 2 * P]

        w_in = m.sem("w_in")
        consts = m.sem("consts")
        rw_turned = m.sem("rw_turned")
        rwT_ready = m.sem("rwT_ready")
        rank_ready = m.sem("rank_ready")
        dve_own = m.sem("dve_own")
        var_ready = m.sem("var_ready")
        rstd_ready = m.sem("rstd_ready")
        xn_ready = m.sem("xn_ready")
        turned = m.sem("turned")
        xnT_ready = m.sem("xnT_ready")
        logits = m.sem("logits")
        lg_out = m.sem("lg_out")
        lg_less = m.sem("lg_less")
        exp_ready = m.sem("exp_ready")
        weights = m.sem("weights")
        val_ready = m.sem("val_ready")
        val_turned = m.sem("val_turned")
        val_out = m.sem("val_out")
        gated = m.sem("gated")
        silu_ready = m.sem("silu_ready")
        hh_ready = m.sem("hh_ready")
        down = m.sem("down")
        added = m.sem("added")
        stored = [m.sem(f"stored{s}") for s in range(2)]
        block = ctx.enter_context(nc.Block())
        FIRST, LAST = 2, N - 2

        @block.sync
        def _(sp):
            sp.dma_start(rw[:, :], io["router_w"]).then_inc(w_in, 16)
            sp.dma_start(wgu[:, :, :], io["ws_gate_up"].rearrange("(c p) n -> p c n", p=P)).then_inc(w_in, 16)
            sp.dma_start(wd[:, :, :], io["ws_down"].rearrange("(c p) n -> p c n", p=FP)).then_inc(w_in, 16)
            dst = table[0:TOK, :].rearrange("(h t p) c -> p h t c", p=P, h=2)

            def group(n, s, turn, ahead):
                sp.wait_ge(weights, v(n + 1))
                for h in range(2):
                    sp.dma_start(dst[:, h, bass.ds(v(n * 2), 2), :], rows[:, s, 2 * h:2 * h + 2, :])\
                      .then_inc(stored[s], 16)
            turns(sp, group, N, 2, FIRST, LAST)
            for s in range(2):
                sp.wait_ge(stored[s], 16 * 2 * N // 2)

        @block.gpsimd
        def _(pool):
            pool.memset(mhalf[:, :], -0.5).then_inc(consts, 1)
            pool.iota(ranki[:, :], [[-P, TILES]], base=TOK, channel_multiplier=-1).then_inc(consts, 1)

            def group(n, s, turn, ahead):
                pool.wait_ge(var_ready, v(n + 1))
                pool.tensor_tensor(rstd[:, :], mom[:, 5, :], mhalf[:, :], ALU.pow).then_inc(rstd_ready, 1)
            turns(pool, group, N, 2, FIRST, LAST)

        @block.scalar
        def _(act):
            def copy_xnT(n):
                act.wait_ge(turned, v(n + 1))
                for c in range(DC):
                    act.activation(xnT[:, c, :], pT[:, c, :], ACT.Copy).then_inc(xnT_ready, 1)

            def group(n, s, turn, ahead):
                act.wait_ge(lg_less, v(n + 1))
                if not early(n, 1):
                    act.wait_ge(weights, v(n))
                act.activation(ex[:, :, :], less[:, :, :], ACT.Exp).then_inc(exp_ready, 1)
                for c in range(FC):
                    act.wait_ge(gated, v(n * 4 + (c + 1)))
                    if not early(n, 1):
                        act.wait_ge(hh_ready, v(n * 2))
                    act.activation(sg[:, c, :], pG[0:FP, c, :], ACT.Silu).then_inc(silu_ready, 1)
                if ahead:
                    act.wait_ge(gated, v(n * 4 + 4))
                    copy_xnT(n + 1)

            copy_xnT(0)
            turns(act, group, N, 2, FIRST, LAST)

        @block.vector
        def _(dve):
            dve.wait_ge(consts, 2)
            dve.tensor_copy(rank[:, :], ranki[:, :]).then_inc(rank_ready, 1)
            dve.wait_ge(rw_turned, 1)
            dve.tensor_copy(rwT[:, :, :], pT[:, :, 0:EXPERTS]).then_inc(rwT_ready, 1)
            dve.wait_ge(rank_ready, 1)

            def norm(n, s, turn):
                own = Chain(dve, dve_own, n * OWN_LN)
                layer_norm_stats(dve, own, [tile_of(x_sb, v(n * 2) + HT * (q // 2) + q % 2) for q in range(G)],
                                 stats, mom, var_ready)
                dve.wait_ge(rstd_ready, v(n + 1))
                if not early(n, 2):
                    dve.wait_ge(stored[s], v(turn * 32))
                for q in range(G):
                    dve.tensor_scalar(rows[:, s, q, 0:D], tile_of(x_sb, v(n * 2) + HT * (q // 2) + q % 2),
                                      mom[:, 4, q:q + 1], rstd[:, q:q + 1], ALU.subtract, ALU.mult).then_inc(xn_ready, 1)

            OWN_LN = 10
            route_own = m.sem("route_own")
            OWN_ROUTE = 2 + 4 + 4 + 1 + 3

            def group(n, s, turn, ahead):
                if ahead:
                    norm(n + 1, (s + 1) % 2, turn + (s + 1) // 2)
                own = Chain(dve, route_own, n * OWN_ROUTE)
                dve.wait_ge(logits, v(n + 1))
                own(dve.tensor_copy(lg[:, :, :].rearrange("p g e -> p (g e)"), LG))
                own.settle()
                own(dve.tensor_reduce(mx[:, :], lg[:, :, :], AX.X, ALU.max))
                for q in range(G):
                    own(dve.max(top[:, q, :], lg[:, q, :]))
                own.settle()
                if not early(n, 1):
                    dve.wait_ge(exp_ready, v(n))
                dve.tensor_tensor(less[:, :, :], lg[:, :, :],
                                  mx[:, :].rearrange("p (g a) -> p g a", a=1).to_broadcast([P, G, EXPERTS]),
                                  ALU.subtract).then_inc(lg_less, 1)
                for q in range(G):
                    own(dve.match_replace(left[:, q, :], top[:, q, :], lg[:, q, :], NEG))
                own.settle()
                own(dve.tensor_tensor(mask[:, :, :], left[:, :, :], lg[:, :, :], ALU.not_equal))
                own.settle()
                if not early(n, 1):
                    dve.wait_ge(val_turned, v(n))
                rk = rank[:, :].rearrange("p (h t) -> p h t", h=2)[:, :, bass.ds(v(n * 2), 2)]
                dve.tensor_tensor(val[:, :, :, :].rearrange("p t h e -> p h t e"),
                                  mask[:, :, :].rearrange("p (h t) e -> p h t e", h=2),
                                  rk.rearrange("p h (t a) -> p h t a", a=1).to_broadcast([P, 2, 2, EXPERTS]),
                                  ALU.mult).then_inc(val_ready, 1)
                dve.wait_ge(exp_ready, v(n + 1))
                dve.wait_ge(val_ready, v(n + 1))
                own(dve.tensor_tensor(exm[:, :, :], ex[:, :, :], mask[:, :, :], ALU.mult))
                own.settle()
                own(dve.tensor_reduce(den[:, :], exm[:, :, :], AX.X, ALU.add))
                own.settle()
                own(dve.reciprocal(rden[:, :], den[:, :]))
                own.settle()
                assert own.n == OWN_ROUTE
                dve.tensor_tensor(rows[:, s, :, D:ROW], exm[:, :, :],
                                  rden[:, :].rearrange("p (g a) -> p g a", a=1).to_broadcast([P, G, EXPERTS]),
                                  ALU.mult).then_inc(weights, 1)
                dve.wait_ge(val_turned, v(n + 1))
                dve.tensor_copy(order[:, bass.ds(v(n * 256), 256)], VT).then_inc(val_out, 1)
                for c in range(FC):
                    dve.wait_ge(silu_ready, v(n * 2 + (c + 1)))
                    dve.wait_ge(gated, v(n * 4 + (c + 3)))
                    if not early(n, 1):
                        dve.wait_ge(down, v(n * 4))
                    dve.tensor_tensor(hh[:, c, :], sg[:, c, :], pG[0:FP, 2 + c, :], ALU.mult).then_inc(hh_ready, 1)
                for q in range(G):
                    dve.wait_ge(down, v(n * 4 + (q + 1)))
                    row = tile_of(x_sb, v(n * 2) + HT * (q // 2) + q % 2)
                    dve.tensor_tensor(row, row, pD[:, (q % 2) * D:(q % 2 + 1) * D], ALU.add).then_inc(added, 1)

            norm(0, 0, 0)
            turns(dve, group, N, 2, FIRST, LAST)
            dve.wait_ge(added, 4 * N)
            dve.wait_ge(val_out, N)
            dve.wait_ge(weights, N)

        @block.tensor
        def _(pe):
            pe.wait_ge(w_in, 48)
            for c in range(DC):
                mm = pe.transpose(pT[:, c, 0:EXPERTS], rw[:, c * P:(c + 1) * P], ident[0:EXPERTS, 0:EXPERTS])
            mm.then_inc(rw_turned, 1)
            pe.wait_ge(rwT_ready, 1)

            def turn_group(n, s):
                pe.wait_ge(xn_ready, v(n * 4 + 4))
                if not early(n, 1):
                    pe.wait_ge(xnT_ready, v(n * 2))
                for c in range(DC):
                    for q in range(G):
                        mm = pe.transpose(pT[:, c, q * P:(q + 1) * P], rows[:, s, q, c * P:(c + 1) * P], ident[:, :])
                mm.then_inc(turned, 1)

            def group(n, s, turn, ahead):
                pe.wait_ge(xnT_ready, v(n * 2 + 2))
                if not early(n, 1):
                    pe.wait_ge(val_out, v(n))
                for q in range(G):
                    for c in range(DC):
                        mm = pe.matmul(LG[:, q * EXPERTS:(q + 1) * EXPERTS], xnT[:, c, q * P:(q + 1) * P],
                                       rwT[:, c, :], start=(c == 0), stop=(c == DC - 1))
                mm.then_inc(logits, 1)
                for f in range(2 * FC):
                    if not early(n, 1):
                        pe.wait_ge(hh_ready, v(n * 2))
                    for c in range(DC):
                        mm = pe.matmul(pG[0:FP, f, :], wgu[:, c, f * FP:(f + 1) * FP], xnT[:, c, :],
                                       start=(c == 0), stop=(c == DC - 1))
                    mm.then_inc(gated, 1)
                if ahead:
                    turn_group(n + 1, (s + 1) % 2)
                pe.wait_ge(val_ready, v(n + 1))
                for j in range(2):
                    mm = pe.transpose(VT[:, j * P:(j + 1) * P], val[:, j, :, :].rearrange("p h e -> p (h e)"),
                                      ident[:, :])
                mm.then_inc(val_turned, 1)
                pe.wait_ge(hh_ready, v(n * 2 + 2))
                for q in range(G):
                    if q >= 1:
                        pe.wait_ge(added, v(n * 4 + q))
                    elif not early(n, 1):
                        pe.wait_ge(added, v(n * 4))
                    for c in range(FC):
                        mm = pe.matmul(pD[:, (q % 2) * D:(q % 2 + 1) * D], hh[:, c, q * P:(q + 1) * P], wd[:, c, :],
                                       start=(c == 0), stop=(c == FC - 1))
                    mm.then_inc(down, 1)

            turn_group(0, 0)
            turns(pe, group, N, 2, FIRST, LAST)


def phase_slots(nc, tag, ident, order, ids):
    with ExitStack() as ctx:
        m = Mem(nc, ctx, tag)
        firsts = m.sb("firsts", [P, CAP])
        both = m.sb("both", [EXPERTS, 2 * CAP])
        slots = m.sb("slots", [EXPERTS, CAP])
        sloti = m.sb("sloti", [P, 1], I32)
        slotf = m.sb("slotf", [P, 1])
        found = m.sb("found", [P, EXPERTS])
        empty = m.sb("empty", [P, EXPERTS])
        pI = m.ps("pI", [P, BANK])
        consts = m.sem("consts")
        own_sem = m.sem("own")
        moved = m.sem("moved")
        listed = m.sem("listed")
        turned = m.sem("turned")
        block = ctx.enter_context(nc.Block())

        @block.gpsimd
        def _(pool):
            pool.iota(sloti[:, :], [[0, 1]], base=0, channel_multiplier=1).then_inc(consts, 1)

        @block.sync
        def _(sp):
            sp.wait_ge(listed, 1)
            sp.dma_start(both[:, CAP:2 * CAP], firsts[EXPERTS:P, :]).then_inc(moved, 16)

        @block.vector
        def _(dve):
            own = Chain(dve, own_sem)

            def largest(out, src, last):
                for r in range(CAP // TOP):
                    own(dve.max(out[:, r * TOP:(r + 1) * TOP], src))
                    own.settle()
                    if r < CAP // TOP - 1:
                        own(dve.match_replace(src, out[:, r * TOP:(r + 1) * TOP], src, 0.0))
                        own.settle()

            largest(firsts, order[:, :], False)
            dve.tensor_copy(both[:, 0:CAP], firsts[0:EXPERTS, :]).then_inc(listed, 1)
            dve.wait_ge(listed, 1)
            dve.wait_ge(moved, 16)
            largest(slots, both[:, :], True)
            dve.wait_ge(consts, 1)
            dve.tensor_copy(slotf[:, :], sloti[:, :]).then_inc(listed, 1)
            dve.wait_ge(turned, 1)
            dve.wait_ge(listed, 2)
            own(dve.tensor_scalar(found[:, :], pI[:, 0:EXPERTS], -1.0, float(TOK), ALU.mult, ALU.add))
            own(dve.tensor_scalar(empty[:, :], pI[:, 0:EXPERTS], 0.0, slotf[:, 0:1], ALU.is_equal, ALU.mult))
            own.settle()
            own(dve.tensor_tensor(ids[:, :], found[:, :], empty[:, :], ALU.add))
            own.settle()

        @block.tensor
        def _(pe):
            pe.wait_ge(listed, 2)
            pe.transpose(pI[:, 0:EXPERTS], slots[:, :], ident[0:EXPERTS, 0:EXPERTS]).then_inc(turned, 1)


def phase_experts(nc, io, tag, ident, ids, table, sums):
    R = 6
    LEAD = 4
    HALF = 16 * R // 2
    with ExitStack() as ctx:
        m = Mem(nc, ctx, tag)
        wg = m.sb("wg", [P, R, DC, FF])
        wu = m.sb("wu", [P, R, DC, FF])
        wd = m.sb("wd", [FP, R, FC, D])
        idx = [m.sb(f"idx{s}", [P, 1], I32) for s in range(R)]
        xg = [m.sb(f"xg{s}", [P, ROW]) for s in range(R)]
        zero = m.sb("zero", [P, 1], I32)
        stood = m.sb("stood", [P, 2], I32)
        xT = m.sb("xT", [P, 2, DC * P])
        sg = m.sb("sg", [FP, 2, FC * P])
        hh = m.sb("hh", [FP, 2, FC * P])
        y = [m.sb(f"y{s}", [P, D]) for s in range(R)]
        pX = m.ps("pX", [P, 2, BANK])
        pG = m.ps("pG", [P, 2, BANK])
        pY = m.ps("pY", [P, 2, BANK])

        w_in = [m.sem(f"w_in{s}") for s in range(R)]
        consts = m.sem("consts")
        stands = m.sem("stands")
        idx_ready = m.sem("idx_ready")
        x_in = [m.sem(f"x_in{s}") for s in range(R)]
        turned = m.sem("turned")
        xT_ready = m.sem("xT_ready")
        gated = m.sem("gated")
        silu_ready = m.sem("silu_ready")
        hh_ready = m.sem("hh_ready")
        down = m.sem("down")
        y_ready = m.sem("y_ready")
        summed = [m.sem(f"summed{s}") for s in range(2)]
        block = ctx.enter_context(nc.Block())
        FIRST = R + 1
        LAST = FIRST + (EXPERTS - FIRST - LEAD) // R * R

        @block.sync
        def _(sp):
            def expert(n, s, turn, ahead):
                if not early(n, R):
                    sp.wait_ge(down, v(n - (R - 1)))
                for name, tile in (("w_gate", wg), ("w_up", wu)):
                    sp.dma_start(tile[:, s, :, :], io[name][bass.ds(v(n), 1), :, :]
                                 .rearrange("e (p c) f -> p (e c) f", c=DC)).then_inc(w_in[s], 16)
                sp.dma_start(wd[:, s, :, :], io["w_down"][bass.ds(v(n), 1), :, :]
                             .rearrange("e (p c) f -> p (e c) f", c=FC)).then_inc(w_in[s], 16)
            turns(sp, expert, EXPERTS, R, FIRST, LAST)

        @block.gpsimd
        def _(pool):
            pool.memset(zero[:, :], 0).then_inc(consts, 1)
            pool.wait_ge(consts, 1)

            def stand(k):
                return pool.tensor_tensor(stood[:, k:k + 1], zero[:, :], zero[:, :], ALU.add)

            def gather(n, s, turn):
                pool.tensor_tensor(idx[s][:, :], ids[:, bass.ds(v(n), 1)], zero[:, :], ALU.add).then_inc(idx_ready, 1)
                pool.wait_ge(idx_ready, v(n + 1))
                if not early(n, R):
                    pool.wait_ge(y_ready, v(n - (R - 1)))
                stand(0)
                pool.indirect_dma_start(out=xg[s][:, :], out_offset=None, in_=table[:, :],
                                        in_offset=bass.IndirectOffsetOnAxis(ap=idx[s][:, 0:1], axis=0))\
                    .then_inc(x_in[s], 16)

            def expert(n, s, turn, ahead):
                if not early(n, 2):
                    pool.wait_ge(summed[s % 2], v(turn * HALF + 16 * (s // 2)))
                if ahead >= LEAD:
                    gather(n + LEAD, (s + LEAD) % R, turn + (s + LEAD) // R)
                pool.wait_ge(y_ready, v(n + 1))
                if not early(n, 1):
                    pool.wait_ge(stands, v(n))
                stand(1).then_inc(stands, 1)
                pool.indirect_dma_start(out=sums[s % 2][:, :],
                                        out_offset=bass.IndirectOffsetOnAxis(ap=idx[s][:, 0:1], axis=0),
                                        in_=y[s][:, :], in_offset=None, compute_op=ALU.add)\
                    .then_inc(summed[s % 2], 16)

            for n in range(LEAD):
                gather(n, n, 0)
            turns(pool, expert, EXPERTS, R, FIRST, LAST)
            for q in range(2):
                pool.wait_ge(summed[q], 16 * EXPERTS // 2)

        @block.scalar
        def _(act):
            def copy_x(n, q):
                act.wait_ge(turned, v(n + 1))
                if not early(n, 2):
                    act.wait_ge(gated, v(n - 1))
                act.activation(xT[:, q, :], pX[:, q, 0:DC * P], ACT.Copy).then_inc(xT_ready, 1)

            def expert(n, s, turn, ahead):
                if ahead:
                    copy_x(n + 1, (s + 1) % 2)
                act.wait_ge(gated, v(n + 1))
                if not early(n, 2):
                    act.wait_ge(hh_ready, v(n - 1))
                act.activation(sg[:, s % 2, :], pG[0:FP, s % 2, 0:FC * P], ACT.Silu).then_inc(silu_ready, 1)

            copy_x(0, 0)
            turns(act, expert, EXPERTS, R, FIRST, LAST)

        @block.vector
        def _(dve):
            def weigh(n, s, turn):
                dve.wait_ge(down, v(n + 1))
                if not early(n, R):
                    dve.wait_ge(summed[s % 2], v(turn * HALF + (16 * (s // 2 + 1) - HALF)))
                dve.tensor_scalar(y[s][:, :], pY[:, s % 2, 0:D], xg[s][:, bass.ds(v(n + D), 1)], None,
                                  ALU.mult).then_inc(y_ready, 1)

            def expert(n, s, turn, ahead):
                dve.wait_ge(silu_ready, v(n + 1))
                if not early(n, 2):
                    dve.wait_ge(down, v(n - 1))
                dve.tensor_tensor(hh[:, s % 2, :], sg[:, s % 2, :], pG[0:FP, s % 2, FC * P:2 * FC * P],
                                  ALU.mult).then_inc(hh_ready, 1)
                if not early(n, 1):
                    weigh(n - 1, (s - 1) % R, turn + (s - 1) // R)

            turns(dve, expert, EXPERTS, R, FIRST, LAST)
            weigh(EXPERTS - 1, (EXPERTS - 1) % R, (EXPERTS - 1) // R)

        @block.tensor
        def _(pe):
            def turn_x(n, s, turn):
                pe.wait_ge(x_in[s], v(turn * 16 + 16))
                if not early(n, 2):
                    pe.wait_ge(xT_ready, v(n - 1))
                cols = xg[s][:, 0:D].rearrange("t (p c) -> t c p", c=DC)
                for c in range(DC):
                    mm = pe.transpose(pX[:, s % 2, c * P:(c + 1) * P], cols[:, c, :], ident[:, :])
                mm.then_inc(turned, 1)

            def down_product(n, s):
                pe.wait_ge(hh_ready, v(n + 1))
                if not early(n, 2):
                    pe.wait_ge(y_ready, v(n - 1))
                for c in range(FC):
                    mm = pe.matmul(pY[:, s % 2, 0:D], hh[:, s % 2, c * P:(c + 1) * P], wd[:, s, c, :],
                                   start=(c == 0), stop=(c == FC - 1))
                mm.then_inc(down, 1)

            def expert(n, s, turn, ahead):
                if ahead:
                    turn_x(n + 1, (s + 1) % R, turn + (s + 1) // R)
                pe.wait_ge(xT_ready, v(n + 1))
                pe.wait_ge(w_in[s], v(turn * 48 + 48))
                if not early(n, 2):
                    pe.wait_ge(hh_ready, v(n - 1))
                for k, w in enumerate((wg, wu)):
                    cols = w[:, s, :, :].rearrange("p c (f k) -> p c k f", k=FC)
                    for f in range(FC):
                        for c in range(DC):
                            at = (FC * k + f) * P
                            mm = pe.matmul(pG[0:FP, s % 2, at:at + P], cols[:, c, f, :],
                                           xT[:, s % 2, c * P:(c + 1) * P], start=(c == 0), stop=(c == DC - 1))
                mm.then_inc(gated, 1)
                if not early(n, 1):
                    down_product(n - 1, (s - 1) % R)

            turn_x(0, 0, 0)
            turns(pe, expert, EXPERTS, R, FIRST, LAST)
            down_product(EXPERTS - 1, (EXPERTS - 1) % R)


def phase_merge(nc, tag, x_sb, sums, out):
    with ExitStack() as ctx:
        m = Mem(nc, ctx, tag)
        part = m.sb("part", [P, 2, 2, GT, D])
        s_in = [m.sem(f"s_in{s}") for s in range(2)]
        added = m.sem("added")
        stored = m.sem("stored")
        block = ctx.enter_context(nc.Block())
        FIRST, LAST = 2, GROUPS - 2

        def group_of(a, n):
            return a[:, bass.ds(v(n * GT), GT), :]

        @block.sync
        def _(sp):
            def load(n, s):
                if not early(n, 2):
                    sp.wait_ge(added, v((n - 1) * 2))
                for q in range(2):
                    src = sums[q][0:TOK, :].rearrange("(t p) d -> p t d", p=P)
                    sp.dma_start(part[:, s, q, :, :], group_of(src, n)).then_inc(s_in[s], 16)

            def group(n, s, turn, ahead):
                if ahead:
                    load(n + 1, (s + 1) % 2)
                if out is not None:
                    sp.wait_ge(added, v(n * 2 + 2))
                    dst = out.rearrange("b (t p) d -> p (b t) d", p=P)
                    sp.dma_start(group_of(dst, n), group_of(x_sb, n)).then_inc(stored, 16)

            load(0, 0)
            turns(sp, group, GROUPS, 2, FIRST, LAST)
            if out is not None:
                sp.wait_ge(stored, 16 * GROUPS)

        @block.vector
        def _(dve):
            def group(n, s, turn, ahead):
                dve.wait_ge(s_in[s], v(turn * 32 + 32))
                for q in range(2):
                    if q:
                        dve.wait_ge(added, v(n * 2 + 1))
                    row = group_of(x_sb, n)
                    dve.tensor_tensor(row, row, part[:, s, q, :, :], ALU.add).then_inc(added, 1)
            turns(dve, group, GROUPS, 2, FIRST, LAST)
            dve.wait_ge(added, 2 * GROUPS)


def ffn(nc, io, tag, x_sb, ident, table, sums, out):
    with ExitStack() as ctx:
        m = Mem(nc, ctx, tag)
        order = m.sb("order", [P, TOK // 2])
        ids = m.sb("ids", [P, EXPERTS], I32)
        phase_route(nc, io, tag + "r", x_sb, ident, table, order)
        phase_slots(nc, tag + "s", ident, order, ids)
        phase_experts(nc, io, tag + "e", ident, ids, table, sums)
        phase_merge(nc, tag + "m", x_sb, sums, out)


STATES, DT_RANK = 16, 64
BC = 2 * STATES


def phase_ssm_in(nc, io, tag, x_sb, ident, xnT, delta, du, bc3, negA, dcol):
    with ExitStack() as ctx:
        m = Mem(nc, ctx, tag)
        wdt = m.sb("wdt", [P, DC, DT_RANK])
        wbc = m.sb("wbc", [P, DC, 3 * BC])
        wdp = m.sb("wdp", [DT_RANK, D])
        bcol = m.sb("bcol", [P, DC])
        alog = m.sb("alog", [P, DC, STATES])
        stats = m.sb("stats", [P, GT, 6])
        mom = m.sb("mom", [P, 6, GT])
        mhalf = m.sb("mhalf", [P, GT])
        rstd = m.sb("rstd", [P, GT])
        xn = m.sb("xn", [P, GT, D])
        low = m.sb("low", [DT_RANK, GROUP])
        bc_hi = m.sb("bc_hi", [3 * BC, GROUP], BF16)
        bc_mid = m.sb("bc_mid", [3 * BC, GROUP], BF16)
        bc_rest = m.sb("bc_rest", [3 * BC, GROUP])
        size = m.sb("size", [P, DC, GROUP])
        pos = m.sb("pos", [P, DC, GROUP])
        e = m.sb("e", [P, DC, GROUP])
        ln = m.sb("ln", [P, DC, GROUP])
        e1 = m.sb("e1", [P, DC, GROUP])
        lost = m.sb("lost", [P, DC, GROUP])
        fixed = m.sb("fixed", [P, DC, GROUP])

        pT = m.ps("pT", [P, DC, BANK])
        pL = m.ps("pL", [P, BANK])
        pB = m.ps("pB", [P, BANK])
        pD = m.ps("pD", [P, DC, BANK])

        w_in = m.sem("w_in")
        a_ready = m.sem("a_ready")
        consts = m.sem("consts")
        dve_own = m.sem("dve_own")
        var_ready = m.sem("var_ready")
        rstd_ready = m.sem("rstd_ready")
        xn_ready = m.sem("xn_ready")
        turned = m.sem("turned")
        xnT_ready = m.sem("xnT_ready")
        projected = m.sem("projected")
        low_ready = m.sem("low_ready")
        hi_ready = m.sem("hi_ready")
        hi_placed = m.sem("hi_placed")
        bc_own = m.sem("bc_own")
        bc_ready = m.sem("bc_ready")
        dt_done = m.sem("dt_done")
        size_ready = m.sem("size_ready")
        pos_ready = m.sem("pos_ready")
        e_ready = m.sem("e_ready")
        ln_ready = m.sem("ln_ready")
        soft_own = m.sem("soft_own")
        delta_ready = m.sem("delta_ready")
        du_ready = m.sem("du_ready")
        block = ctx.enter_context(nc.Block())
        FIRST, LAST = 2, GROUPS - 2

        def cols(a, n):
            at = bass.ds(v(n * GROUP), GROUP)
            return a[:, :, at] if len(a.shape) == 3 else a[:, at]

        @block.sync
        def _(sp):
            sp.dma_start(wdt[:, :, :], io["W_dt"].rearrange("(c p) r -> p c r", p=P)).then_inc(w_in, 16)
            sp.dma_start(wdp[:, :], io["W_dtproj"]).then_inc(w_in, 16)
            with nc.allow_non_contiguous_dma(reason="short rows of small weights"):
                for r in range(3):
                    sp.dma_start(wbc[:, :, BC * r:BC * r + BC],
                                 io["W_bc"].rearrange("(c p) n -> p c n", p=P)).then_inc(w_in, 16)
                sp.dma_start(bcol[:, :], io["b_dtproj"].rearrange("(c p) -> p c", p=P)).then_inc(w_in, 16)
                sp.dma_start(dcol[:, :], io["D_param"].rearrange("(c p) -> p c", p=P)).then_inc(w_in, 16)
                sp.dma_start(alog[:, :, :], io["A_log"].rearrange("(c p) n -> p c n", p=P)).then_inc(w_in, 16)

        @block.gpsimd
        def _(pool):
            pool.memset(mhalf[:, :], -0.5).then_inc(consts, 1)

            def product(n):
                pool.wait_ge(delta_ready, v(n + 1))
                pool.wait_ge(xnT_ready, v(n * 2 + 2))
                pool.tensor_tensor(cols(du, n), cols(delta, n), cols(xnT, n), ALU.mult).then_inc(du_ready, 1)

            def group(n, s, turn, ahead):
                pool.wait_ge(var_ready, v(n + 1))
                pool.tensor_tensor(rstd[:, :], mom[:, 5, :], mhalf[:, :], ALU.pow).then_inc(rstd_ready, 1)
                if not early(n, 1):
                    product(n - 1)
            turns(pool, group, GROUPS, 2, FIRST, LAST)
            product(GROUPS - 1)
            pool.wait_ge(du_ready, GROUPS)

        @block.scalar
        def _(act):
            act.wait_ge(w_in, 16 * 8)
            act.activation(alog[:, :, :], alog[:, :, :], ACT.Exp).then_inc(a_ready, 1)

            def copy_xnT(n):
                act.wait_ge(turned, v(n + 1))
                act.activation(cols(xnT, n), pT[:, :, :], ACT.Copy).then_inc(xnT_ready, 2)

            def group(n, s, turn, ahead):
                act.wait_ge(projected, v(n * 2 + 1))
                if not early(n, 1):
                    act.wait_ge(dt_done, v(n))
                act.activation(low[:, :], pL[0:DT_RANK, :], ACT.Copy).then_inc(low_ready, 1)
                act.wait_ge(projected, v(n * 2 + 2))
                if not early(n, 1):
                    act.wait_ge(bc_ready, v(n * 2))
                act.activation(bc_hi[:, :], pB[0:3 * BC, :], ACT.Copy).then_inc(hi_ready, 1)
                act.wait_ge(hi_ready, v(n + 1))
                act.activation(cols(bc3, n)[0:BC, :], bc_hi[0:BC, :], ACT.Copy).then_inc(hi_placed, 1)
                act.wait_ge(dt_done, v(n + 1))
                if not early(n, 1):
                    act.wait_ge(e_ready, v(n))
                for c in range(DC):
                    act.activation(size[:, c, :], pD[:, c, :], ACT.Abs, bias=bcol[:, c:c + 1])\
                       .then_inc(size_ready, 1)
                act.wait_ge(size_ready, v(n * 2 + 2))
                if not early(n, 1):
                    act.wait_ge(delta_ready, v(n))
                act.activation(e[:, :, :], size[:, :, :], ACT.Exp, scale=-1.0).then_inc(e_ready, 1)
                act.wait_ge(e_ready, v(n + 1))
                act.activation(ln[:, :, :], e[:, :, :], ACT.Ln, bias=1.0).then_inc(ln_ready, 1)
                if ahead:
                    copy_xnT(n + 1)

            copy_xnT(0)
            turns(act, group, GROUPS, 2, FIRST, LAST)
            act.wait_ge(xnT_ready, 2 * GROUPS)
            act.wait_ge(hi_placed, GROUPS)

        @block.vector
        def _(dve):
            dve.wait_ge(a_ready, 1)
            dve.tensor_scalar(negA[:, :, :], alog[:, :, :], -1.0, None, ALU.mult).then_inc(a_ready, 1)
            dve.wait_ge(consts, 1)
            OWN_LN, OWN_BC, OWN_SOFT = 10, 2, 3

            def norm(n):
                own = Chain(dve, dve_own, n * OWN_LN)
                layer_norm_stats(dve, own, [tile_of(x_sb, v(n * GT) + j) for j in range(GT)], stats, mom, var_ready)
                assert own.n == OWN_LN
                dve.wait_ge(rstd_ready, v(n + 1))
                if not early(n, 1):
                    dve.wait_ge(turned, v(n))
                for j in range(GT):
                    dve.tensor_scalar(xn[:, j, :], tile_of(x_sb, v(n * GT) + j), mom[:, 4, j:j + 1], rstd[:, j:j + 1],
                                      ALU.subtract, ALU.mult).then_inc(xn_ready, 1)

            def group(n, s, turn, ahead):
                if ahead:
                    norm(n + 1)
                own = Chain(dve, bc_own, n * OWN_BC)
                dve.wait_ge(hi_ready, v(n + 1))
                if not early(n, 1):
                    dve.wait_ge(bc_ready, v(n * 2))
                own(dve.tensor_tensor(bc_rest[:, :], pB[0:3 * BC, :], bc_hi[:, :], ALU.subtract))
                own.settle()
                own(dve.tensor_copy(bc_mid[:, :], bc_rest[:, :]))
                own.settle()
                dve.tensor_copy(cols(bc3, n)[BC:2 * BC, :], bc_mid[BC:2 * BC, :]).then_inc(bc_ready, 1)
                dve.tensor_tensor(cols(bc3, n)[2 * BC:3 * BC, :], bc_rest[2 * BC:3 * BC, :], bc_mid[2 * BC:3 * BC, :],
                                  ALU.subtract).then_inc(bc_ready, 1)
                dve.wait_ge(size_ready, v(n * 2 + 2))
                if not early(n, 1):
                    dve.wait_ge(delta_ready, v(n))
                for c in range(DC):
                    dve.tensor_scalar(pos[:, c, :], pD[:, c, :], bcol[:, c:c + 1], 0.0, ALU.add, ALU.max)\
                       .then_inc(pos_ready, 1)
                own = Chain(dve, soft_own, n * OWN_SOFT)
                dve.wait_ge(e_ready, v(n + 1))
                own(dve.tensor_scalar(e1[:, :, :], e[:, :, :], 1.0, -1.0, ALU.add, ALU.add))
                own.settle()
                own(dve.tensor_tensor(lost[:, :, :], e[:, :, :], e1[:, :, :], ALU.subtract))
                own.settle()
                dve.wait_ge(ln_ready, v(n + 1))
                own(dve.tensor_tensor(fixed[:, :, :], ln[:, :, :], lost[:, :, :], ALU.add))
                own.settle()
                dve.wait_ge(pos_ready, v(n * 2 + 2))
                dve.tensor_tensor(cols(delta, n), fixed[:, :, :], pos[:, :, :], ALU.add).then_inc(delta_ready, 1)

            norm(0)
            turns(dve, group, GROUPS, 2, FIRST, LAST)
            dve.wait_ge(delta_ready, GROUPS)
            dve.wait_ge(bc_ready, 2 * GROUPS)
            dve.wait_ge(a_ready, 2)

        @block.tensor
        def _(pe):
            pe.wait_ge(w_in, 16 * 8)

            def turn_group(n):
                pe.wait_ge(xn_ready, v(n * 4 + 4))
                if not early(n, 1):
                    pe.wait_ge(xnT_ready, v(n * 2))
                for c in range(DC):
                    for q in range(GT):
                        mm = pe.transpose(pT[:, c, q * P:(q + 1) * P], xn[:, q, c * P:(c + 1) * P], ident[:, :])
                mm.then_inc(turned, 1)

            def group(n, s, turn, ahead):
                pe.wait_ge(xnT_ready, v(n * 2 + 2))
                if not early(n, 1):
                    pe.wait_ge(low_ready, v(n))
                for c in range(DC):
                    mm = pe.matmul(pL[0:DT_RANK, :], wdt[:, c, :], cols(xnT, n)[:, c, :],
                                   start=(c == 0), stop=(c == DC - 1))
                mm.then_inc(projected, 1)
                if not early(n, 1):
                    pe.wait_ge(bc_ready, v(n * 2))
                for c in range(DC):
                    mm = pe.matmul(pB[0:3 * BC, :], wbc[:, c, :], cols(xnT, n)[:, c, :],
                                   start=(c == 0), stop=(c == DC - 1))
                mm.then_inc(projected, 1)
                pe.wait_ge(low_ready, v(n + 1))
                if not early(n, 1):
                    pe.wait_ge(pos_ready, v(n * 2))
                for c in range(DC):
                    mm = pe.matmul(pD[:, c, :], wdp[:, c * P:(c + 1) * P], low[:, :], start=True, stop=True)
                mm.then_inc(dt_done, 1)
                if ahead:
                    turn_group(n + 1)

            turn_group(0)
            turns(pe, group, GROUPS, 2, FIRST, LAST)


def phase_scan(nc, tag, ident, xnT, delta, du, bc3, negA, dcol):
    SPAN = 2 * GROUP
    SPANS = SEQ // SPAN
    STEPS = SPANS * STATES
    with ExitStack() as ctx:
        m = Mem(nc, ctx, tag)
        sel = m.sb("sel", [3 * BC, BC, P], BF16)
        b_sb = [m.sb(f"b{s}", [P, SPAN]) for s in range(2)]
        decay = [m.sb(f"decay{s}", [P, DC, SPAN]) for s in range(2)]
        bh = [m.sb(f"bh{s}", [P, DC, SPAN]) for s in range(2)]
        hc = [m.sb(f"hc{s}", [P, DC, SPAN]) for s in range(2)]
        carry = m.sb("carry", [P, DC, STATES])
        begun = m.sb("begun", [P, 8])
        pB = m.ps("pB", [P, 2, BANK])
        pC = m.ps("pC", [P, 2, BANK])
        pY = m.ps("pY", [P, DC, 2, BANK])

        consts = m.sem("consts")
        b_spread = m.sem("b_spread")
        c_spread = m.sem("c_spread")
        b_ready = m.sem("b_ready")
        decay_ready = m.sem("decay_ready")
        bx_ready = m.sem("bx_ready")
        h_ready = m.sem("h_ready")
        kept = m.sem("kept")
        hc_ready = m.sem("hc_ready")
        summed = m.sem("summed")
        y_ready = m.sem("y_ready")
        from_one = (b_ready, bx_ready, h_ready, kept, hc_ready, summed, y_ready)
        block = ctx.enter_context(nc.Block())

        def col(b, k):
            return bass.ds(b * SEQ + (k // STATES) * SPAN, SPAN)

        def begin(b, k, back=0):
            return b * STEPS + (max(k - back, 0) + 1)

        def begin2(b, k, back=0):
            return b * (2 * STEPS) + (2 * max(k - back, 0) + 1)

        @block.gpsimd
        def _(pool):
            pool.memset(sel[:, :, :], 0.0).then_inc(consts, 1)
            for r in range(3):
                pool.wait_ge(consts, 1 + r)
                pool.affine_select(out=sel[:, :, :], in_=sel[:, :, :], compare_op=ALU.not_equal, fill=1.0,
                                   base=-BC * r, pattern=[[-1, BC], [0, P]], channel_multiplier=1)\
                    .then_inc(consts, 1)
            for i, sem in enumerate(from_one):
                pool.memset(begun[:, i:i + 1], 0.0).then_inc(sem, 1)
            pool.memset(begun[:, 7:8], 0.0).then_inc(consts, 1)
            with pool.Fori(0, BATCH) as b:
                for k in range(STEPS):
                    s = k % 2
                    pool.wait_ge(b_ready, begin(b, k + 1))
                    pool.wait_ge(hc_ready, begin(b, k, 1))
                    pool.tensor_tensor(bh[s][:, :, :], du[:, :, col(b, k)],
                                       b_sb[s][:, :].rearrange("p (a n) -> p a n", a=1).to_broadcast([P, DC, SPAN]),
                                       ALU.mult).then_inc(bx_ready, 1)

        @block.scalar
        def _(act):
            act.wait_ge(consts, 5)

            def spread_b(b, k):
                act.wait_ge(b_spread, b * STEPS + k + 1)
                act.wait_ge(bx_ready, begin(b, k, 1))
                act.activation(b_sb[k % 2][:, :], pB[:, :, :].rearrange("p a n -> p (a n)"), ACT.Copy)\
                   .then_inc(b_ready, 1)

            def decays(b, k):
                s, n = k % 2, k % STATES
                for c in range(DC):
                    act.wait_ge(h_ready, begin2(b, k, 1))
                    act.activation(decay[s][:, c, :], delta[:, c, col(b, k)], ACT.Exp,
                                   scale=negA[:, c, n:n + 1]).then_inc(decay_ready, 1)

            with act.Fori(0, BATCH) as b:
                spread_b(b, 0)
                decays(b, 0)
                spread_b(b, 1)
                for k in range(STEPS):
                    if k + 1 < STEPS:
                        decays(b, k + 1)
                    if k + 2 < STEPS:
                        spread_b(b, k + 2)

        @block.vector
        def _(dve):
            dve.wait_ge(consts, 5)
            with dve.Fori(0, BATCH) as b:
                for k in range(STEPS):
                    s, n = k % 2, k % STATES
                    for c in range(DC):
                        dve.wait_ge(bx_ready, begin(b, k + 1))
                        dve.wait_ge(decay_ready, b * (2 * STEPS) + (2 * k + c + 1))
                        dve.wait_ge(kept, begin(b, k))
                        dve.tensor_tensor_scan(bh[s][:, c, :], decay[s][:, c, :], bh[s][:, c, :],
                                               0.0 if k < STATES else carry[:, c, n:n + 1],
                                               ALU.mult, ALU.add).then_inc(h_ready, 1)
                    dve.wait_ge(h_ready, begin2(b, k + 1))
                    dve.tensor_copy(carry[:, :, n:n + 1], bh[s][:, :, SPAN - 1:SPAN]).then_inc(kept, 1)
                    dve.wait_ge(c_spread, b * STEPS + k + 1)
                    dve.wait_ge(summed, begin(b, k, 1))
                    c_n = pC[:, :, :].rearrange("p a n -> p (a n)").rearrange("p (b n) -> p b n", b=1)
                    dve.tensor_tensor(hc[s][:, :, :], bh[s][:, :, :], c_n.to_broadcast([P, DC, SPAN]),
                                      ALU.mult).then_inc(hc_ready, 1)
                    if n == STATES - 1:
                        dve.wait_ge(summed, begin(b, k + 1))
                        for c in range(DC):
                            x_c = xnT[:, c, col(b, k)]
                            dve.scalar_tensor_tensor(out=x_c, in0=x_c, scalar=dcol[:, c:c + 1],
                                                     in1=pY[:, c, :, :].rearrange("p a n -> p (a n)"),
                                                     op0=ALU.mult, op1=ALU.add).then_inc(y_ready, 1)
            dve.wait_ge(y_ready, BATCH * SPANS * DC + 1)

        @block.tensor
        def _(pe):
            pe.wait_ge(consts, 5)

            def spread(dst, row, b, k):
                for j in range(2):
                    at = bass.ds(b * SEQ + ((k // STATES) * SPAN + j * GROUP), GROUP)
                    mm = pe.matmul(dst[:, j, :], sel[:, row, :], bc3[:, at], start=True, stop=True)
                return mm

            def spread_b(b, k):
                pe.wait_ge(b_ready, begin(b, k))
                spread(pB, k % STATES, b, k).then_inc(b_spread, 1)

            def total(b, k, between=None):
                s, n = k % 2, k % STATES
                pe.wait_ge(hc_ready, begin(b, k + 1))
                if n == 0:
                    pe.wait_ge(y_ready, b * (SPANS * DC) + (DC * (k // STATES) + 1))
                for c in range(DC):
                    if c and between:
                        spread_b(*between)
                    for j in range(2):
                        mm = pe.matmul(pY[:, c, j, :], ident[:, :], hc[s][:, c, j * GROUP:(j + 1) * GROUP],
                                       start=(n == 0), stop=(n == STATES - 1))
                mm.then_inc(summed, 1)

            with pe.Fori(0, BATCH) as b:
                spread_b(b, 0)
                spread_b(b, 1)
                for k in range(STEPS):
                    pe.wait_ge(hc_ready, begin(b, k))
                    spread(pC, STATES + k % STATES, b, k).then_inc(c_spread, 1)
                    if k:
                        total(b, k - 1, (b, k + 2) if k + 2 < STEPS else None)
                    else:
                        spread_b(b, 2)
                total(b, STEPS - 1)


def phase_ssm_out(nc, tag, x_sb, yT, ident):
    with ExitStack() as ctx:
        m = Mem(nc, ctx, tag)
        y = m.sb("y", [P, 2, DC, 2 * P])
        pY = m.ps("pY", [P, 2, BANK])
        staged = m.sem("staged")
        turned = m.sem("turned")
        added = m.sem("added")
        block = ctx.enter_context(nc.Block())
        PAIRS = TILES // 2

        @block.scalar
        def _(act):
            def pair(n, s, turn, ahead):
                if not early(n, 2):
                    act.wait_ge(turned, v(n - 1))
                act.activation(y[:, s, :, :], yT[:, :, bass.ds(v(n * 2 * P), 2 * P)], ACT.Copy).then_inc(staged, 1)
            turns(act, pair, PAIRS, 2, 2, PAIRS - 2)

        @block.vector
        def _(dve):
            def pair(n, s, turn, ahead):
                dve.wait_ge(turned, v(n + 1))
                rows = x_sb[:, bass.ds(v(n * 2), 2), :]
                dve.tensor_tensor(rows, rows, pY[:, s, :].rearrange("p (t d) -> p t d", t=2), ALU.add)\
                   .then_inc(added, 1)
            turns(dve, pair, PAIRS, 2, 2, PAIRS - 2)
            dve.wait_ge(added, PAIRS)

        @block.tensor
        def _(pe):
            def pair(n, s, turn, ahead):
                pe.wait_ge(staged, v(n + 1))
                if not early(n, 2):
                    pe.wait_ge(added, v(n - 1))
                for t in range(2):
                    for c in range(DC):
                        mm = pe.transpose(pY[:, s, t * D + c * P:t * D + (c + 1) * P],
                                          y[:, s, c, t * P:(t + 1) * P], ident[:, :])
                mm.then_inc(turned, 1)
            turns(pe, pair, PAIRS, 2, 2, PAIRS - 2)


def state_space(nc, io, x_sb, ident):
    with ExitStack() as ctx:
        m = Mem(nc, ctx, "ssm")
        xnT = m.sb("xnT", [P, DC, TOK])
        negA = m.sb("negA", [P, DC, STATES])
        dcol = m.sb("dcol", [P, DC])
        delta = m.sb("delta", [P, DC, TOK])
        du = m.sb("du", [P, DC, TOK])
        bc3 = m.sb("bc3", [3 * BC, TOK], BF16)
        phase_ssm_in(nc, io, "si", x_sb, ident, xnT, delta, du, bc3, negA, dcol)
        phase_scan(nc, "sc", ident, xnT, delta, du, bc3, negA, dcol)
        phase_ssm_out(nc, "so", x_sb, xnT, ident)


def build(nc, io, out):
    q_dram = nc.dram_tensor("query_parts", [3, BATCH * D, SEQ], BF16, kind="Internal").ap()
    k_dram = nc.dram_tensor("key_parts", [3, BATCH * D, SEQ], BF16, kind="Internal").ap()
    table = nc.dram_tensor("token_table", [TOK + P, ROW], F32, kind="Internal").ap()
    sums = [nc.dram_tensor(f"expert_sum{i}", [TOK + P, D], F32, kind="Internal").ap() for i in range(4)]
    with ExitStack() as ctx:
        m = Mem(nc, ctx, "all")
        ident = m.sb("ident", [P, P])
        x_sb = m.sb("x", [P, TILES, D])
        with ExitStack() as outputs:
            a_sb = Mem(nc, outputs, "all").sb("a", [P, BATCH, HEADS, KT, DK])
            with ExitStack() as values:
                v_sb = Mem(nc, values, "all").sb("v", [P, BATCH, HEADS, KT, DK])
                phase_qkv(nc, io, x_sb, v_sb, ident, q_dram, k_dram, sums, table)
                nc.disable_value_cache = True
                phase_attention(nc, v_sb, a_sb, q_dram, k_dram)
            phase_attention_out(nc, io, x_sb, a_sb, ident)
        ffn(nc, io, "f1", x_sb, ident, table, sums[0:2], None)
        state_space(nc, io, x_sb, ident)
        ffn(nc, io, "f2", x_sb, ident, table, sums[2:4], out)


NAMES = {
    "L0_attn_a_": ("x", "WQ", "bQ", "WK", "bK", "WV", "bV", "WO", "bO", "WQr", "WKr"),
    "L0_attn_b_": ("A_log", "D_param", "W_bc", "W_dt", "W_dtproj", "b_dtproj"),
    "L0_ffn_": ("router_w", "w_gate", "w_up", "w_down", "ws_gate_up", "ws_down"),
}


def kernel(**inputs):
    import concourse.bacc as bacc
    from concourse.bass_utils import run_bass_kernel_spmd

    nc = bacc.Bacc("TRN2", target_bir_lowering=False, num_devices=1)
    arrays, io = {}, {}
    for prefix, names in NAMES.items():
        for name in names:
            a = np.ascontiguousarray(inputs[prefix + name])
            arrays[f"in_{name}"] = a
            io[name] = nc.dram_tensor(f"in_{name}", a.shape, mybir.dt.from_np(a.dtype), kind="ExternalInput").ap()
    out = nc.dram_tensor("out_x", (BATCH, SEQ, D), F32, kind="ExternalOutput").ap()
    build(nc, io, out)
    r = run_bass_kernel_spmd(nc, [arrays], core_ids=[0])
    return r.results[0]["out_x"]
```

```python
from contextlib import ExitStack

import numpy as np

import concourse.bass as bass
from concourse import mybir

F32 = mybir.dt.float32
BF16 = mybir.dt.bfloat16
I32 = mybir.dt.int32
U32 = mybir.dt.uint32
ALU = mybir.AluOpType
ACT = mybir.ActivationFunctionType
AX = mybir.AxisListType

P = 128
BATCH, SEQ, D = 2, 2048, 256
TOK = BATCH * SEQ
TILES = TOK // P
DC = D // P
HEADS, DK = 16, 16
GT = 4
GROUP = GT * P
GROUPS = TOK // GROUP
KT = SEQ // P
QC = SEQ // GROUP
LN_EPS = 1e-5
BANK = 512
EXPERTS, TOP, CAP, FF = 64, 8, 128, 192
FC, FP = 2, 96
ROW = D + EXPERTS
NEG = -3.0e38
SPARE = TOK

Q_PARTS = (0, 1, 2, 0, 1, 0)
K_PARTS = (0, 0, 0, 1, 1, 2)
PAIR_ROWS = DK * len(Q_PARTS)
SHIFT_ROWS = 2
ROWS = PAIR_ROWS + SHIFT_ROWS


class Mem:

    def __init__(self, nc, ctx, tag):
        self.nc, self.ctx, self.tag = nc, ctx, tag
        self.sems = []
        ctx.callback(self.clear)

    def sb(self, name, shape, dt=F32):
        return self.ctx.enter_context(self.nc.sbuf_tensor(f"{self.tag}_{name}", shape, dt))

    def ps(self, name, shape, dt=F32):
        return self.ctx.enter_context(self.nc.psum_tensor(f"{self.tag}_{name}", shape, dt))

    def sem(self, name):
        self.sems.append(self.nc.alloc_semaphore(f"{self.tag}_{name}"))
        return self.sems[-1]

    def clear(self):
        if self.sems:
            self.nc.clear_and_free_semaphores(self.sems)
            self.nc.all_engine_barrier()


class Chain:

    def __init__(self, eng, sem, start=0):
        self.eng, self.sem, self.start, self.n = eng, sem, start, 0

    def __call__(self, ins):
        self.n += 1
        return ins.then_inc(self.sem, 1)

    def settle(self):
        self.eng.wait_ge(self.sem, v(self.start + self.n))


class Step:

    def __init__(self, eng, turn, a=1, b=0, held=None):
        self.eng, self.turn, self.a, self.b = eng, turn, a, b
        self.held = {} if held is None else held

    def __mul__(self, k):
        return Step(self.eng, self.turn, self.a * k, self.b * k, self.held)

    def __add__(self, k):
        return Step(self.eng, self.turn, self.a, self.b + k, self.held)

    def __sub__(self, k):
        return self + -k

    __rmul__, __radd__ = __mul__, __add__

    def value(self):
        if self.a not in self.held:
            self.held[self.a] = self.eng.snap(self.turn * self.a)
        return self.held[self.a] + self.b


def v(x):
    return x.value() if isinstance(x, Step) else x


def early(n, k):
    return isinstance(n, int) and n < k


def turns(eng, body, count, ring, first, last):
    assert (last - first) % ring == 0 and first >= 1
    for n in range(first):
        body(n, n % ring, n // ring, count - 1 - n)
    with eng.Fori(0, (last - first) // ring) as i:
        at = Step(eng, i)
        for n in range(first, first + ring):
            body(at * ring + n, n % ring, at + n // ring, count - last)
    for n in range(last, count):
        body(n, n % ring, n // ring, count - 1 - n)


def tile_of(x_sb, t):
    return x_sb[:, bass.ds(t, 1), :].rearrange("p a d -> p (a d)")


def make_identity(eng, tile, done, value):
    eng.memset(tile, 0.0).then_inc(done, 1)
    eng.wait_ge(done, value + 1)
    n = tile.shape[1]
    eng.affine_select(out=tile, in_=tile, compare_op=ALU.not_equal, fill=1.0, base=0,
                      pattern=[[-1, n]], channel_multiplier=1).then_inc(done, 1)


def layer_norm_stats(dve, own, rows, stats, mom, var_ready):
    for j, x in enumerate(rows):
        own(dve.bn_stats(stats[:, j, :], x))
    own.settle()
    own(dve.tensor_tensor(mom[:, 0, :], stats[:, :, 1], stats[:, :, 4], ALU.add))
    own(dve.tensor_tensor(mom[:, 1, :], stats[:, :, 1], stats[:, :, 4], ALU.subtract))
    own(dve.tensor_tensor(mom[:, 2, :], stats[:, :, 2], stats[:, :, 5], ALU.add))
    own.settle()
    own(dve.tensor_tensor(mom[:, 3, :], mom[:, 1, :], mom[:, 1, :], ALU.mult))
    own(dve.tensor_scalar(mom[:, 4, :], mom[:, 0, :], 0.5, None, ALU.mult))
    own(dve.tensor_scalar(mom[:, 2, :], mom[:, 2, :], 1.0 / D, LN_EPS, ALU.mult, ALU.add))
    own.settle()
    dve.scalar_tensor_tensor(out=mom[:, 5, :], in0=mom[:, 3, :], scalar=0.25, in1=mom[:, 2, :],
                             op0=ALU.mult, op1=ALU.add).then_inc(var_ready, 1)


def row_bcast(v, n):
    return v.rearrange("(a n) -> a n", a=1).to_broadcast([P, n])


def phase_qkv(nc, io, x_sb, v_sb, ident, q_dram, k_dram, sums, table):
    with ExitStack() as ctx:
        m = Mem(nc, ctx, "qkv")
        w_sb = {s: m.sb(f"w{s}", [P, DC, D]) for s in "qkv"}
        wT = m.sb("wT", [P, DC, D])
        wr = {s: m.sb(f"wr{s}", [P, P]) for s in "qk"}
        wf = {s: m.sb(f"wf{s}", [P, DC, D]) for s in "qk"}
        bcol = {s: m.sb(f"bcol{s}", [P, DC]) for s in "qk"}
        bf = m.sb("bf", [P, 2, DC])
        bv = m.sb("bv", [P, D])
        stats = m.sb("stats", [P, GT, 6])
        mom = m.sb("mom", [P, 6, GT])
        mhalf = m.sb("mhalf", [P, GT])
        rstd = m.sb("rstd", [P, GT])
        xn = m.sb("xn", [P, GT, D])
        xnT = m.sb("xnT", [P, 2, DC, GROUP])
        full = m.sb("full", [P, 2, GROUP])
        rest = m.sb("rest", [P, 2, GROUP])
        parts = m.sb("parts", [P, 2, 4, 3, GROUP], BF16)
        zeros = m.sb("zeros", [P, ROW])

        pT = m.ps("pT", [P, DC, BANK])
        pQK = m.ps("pQK", [P, 4, BANK])
        pV = m.ps("pV", [P, 2, BANK])

        w_in = m.sem("w_in")
        x_in = m.sem("x_in")
        consts = m.sem("consts")
        cleared = m.sem("cleared")
        blocks = m.sem("blocks")
        wt_done = m.sem("wt_done")
        wt_out = m.sem("wt_out")
        wf_done = m.sem("wf_done")
        wf_out = m.sem("wf_out")
        dve_own = m.sem("dve_own")
        var_ready = m.sem("var_ready")
        rstd_ready = m.sem("rstd_ready")
        xn_ready = m.sem("xn_ready")
        turned = m.sem("turned")
        xnT_ready = m.sem("xnT_ready")
        qk_done = m.sem("qk_done")
        v_done = m.sem("v_done")
        v_out = m.sem("v_out")
        full_ready = m.sem("full_ready")
        part0_ready = m.sem("part0_ready")
        rest_ready = m.sem("rest_ready")
        part1_ready = m.sem("part1_ready")
        parts_ready = m.sem("parts_ready")
        stored = [m.sem(f"stored{s}") for s in range(2)]
        block = ctx.enter_context(nc.Block())

        weights = {"q": io["WQ"], "k": io["WK"], "v": io["WV"]}
        biases = {"q": io["bQ"], "k": io["bK"]}
        ranks = {"q": io["WQr"], "k": io["WKr"]}
        FIRST, LAST = 2, GROUPS - 2

        @block.sync
        def _(sp):
            xs = io["x"].rearrange("b (t p) d -> p (b t) d", p=P)
            for n in range(4):
                sp.dma_start(x_sb[:, 8 * n:8 * n + 8, :], xs[:, 8 * n:8 * n + 8, :]).then_inc(x_in, 16)

            def group(n, s, turn, ahead):
                b, col = v(n) // QC, (v(n) % QC) * GROUP
                for j in range(4):
                    sp.wait_ge(parts_ready, v(n * 4 + (j + 1)))
                    side, c2 = (q_dram, k_dram)[j // 2], j % 2
                    dst = side.rearrange("a (b r) n -> r a b n", b=BATCH)
                    sp.dma_start(dst[c2 * P:(c2 + 1) * P, :, bass.ds(b, 1), bass.ds(col, GROUP)]
                                 .rearrange("r a b n -> r a (b n)"), parts[:, s, j, :, :]).then_inc(stored[s], 16)
            turns(sp, group, GROUPS, 2, FIRST, LAST)
            for q in range(2):
                sp.wait_ge(stored[q], 16 * 4 * GROUPS // 2)

        @block.gpsimd
        def _(pool):
            make_identity(pool, ident[:, :], consts, 0)
            pool.memset(mhalf[:, :], -0.5).then_inc(consts, 1)
            pool.memset(wr["q"][:, :], 0.0).then_inc(consts, 1)
            pool.memset(wr["k"][:, :], 0.0).then_inc(consts, 1)
            pool.memset(zeros[:, :], 0.0).then_inc(consts, 1)

            def rstd_of(n):
                pool.wait_ge(var_ready, v(n + 1))
                pool.tensor_tensor(rstd[:, :], mom[:, 5, :], mhalf[:, :], ALU.pow).then_inc(rstd_ready, 1)

            def group(n, s, turn, ahead):
                if ahead:
                    rstd_of(n + 1)
                for j in range(4):
                    pool.wait_ge(part1_ready, v(n * 4 + (j + 1)))
                    pool.tensor_tensor(parts[:, s, j, 2, :], rest[:, j % 2, :], parts[:, s, j, 1, :],
                                       ALU.subtract).then_inc(parts_ready, 1)
            rstd_of(0)
            turns(pool, group, GROUPS, 2, FIRST, LAST)

        @block.scalar
        def _(act):
            for s in "qkv":
                act.dma_start(w_sb[s][:, :, :], weights[s].rearrange("(c p) n -> p c n", p=P)).then_inc(w_in, 16)
            act.dma_start(bv[:, :], row_bcast(io["bV"], D)).then_inc(w_in, 16)
            with nc.allow_non_contiguous_dma(reason="two bias columns"):
                for s in "qk":
                    act.dma_start(bcol[s][:, :], biases[s].rearrange("(c p) -> p c", p=P)).then_inc(w_in, 16)
            act.wait_ge(consts, 5)
            for s in "qk":
                for h in range(P // DK):
                    act.dma_start(wr[s][DK * h:DK * h + DK, DK * h:DK * h + DK], ranks[s]).then_inc(blocks, 16)
            act.wait_ge(consts, 6)
            for to in sums:
                act.dma_start(to.rearrange("(t p) c -> p t c", p=P),
                              zeros[:, 0:D].rearrange("p (a c) -> p a c", a=1).to_broadcast([P, TILES + 1, D]))\
                   .then_inc(cleared, 16)
            act.dma_start(table[SPARE:SPARE + P, :], zeros[:, :]).then_inc(cleared, 16)

            def copy_xnT(n, s):
                act.wait_ge(turned, v(n + 1))
                if not early(n, 2):
                    act.wait_ge(v_done, v(n * 2 - 2))
                act.activation(xnT[:, s, :, :], pT[:, :, :], ACT.Copy).then_inc(xnT_ready, 1)

            def group(n, s, turn, ahead):
                for j in range(4):
                    act.wait_ge(qk_done, v(n * 4 + (j + 1)))
                    if j >= 2 or not early(n, 1):
                        act.wait_ge(rest_ready, v(n * 4 + (j - 1)))
                    act.activation(full[:, j % 2, :], pQK[:, j, :], ACT.Identity,
                                   bias=bf[:, j // 2, j % 2:j % 2 + 1]).then_inc(full_ready, 1)
                    if not early(n, 2):
                        act.wait_ge(stored[s], v(turn * 64))
                    act.activation(parts[:, s, j, 0, :], pQK[:, j, :], ACT.Identity,
                                   bias=bf[:, j // 2, j % 2:j % 2 + 1]).then_inc(part0_ready, 1)
                if ahead:
                    copy_xnT(n + 1, (s + 1) % 2)
            copy_xnT(0, 0)
            turns(act, group, GROUPS, 2, FIRST, LAST)
            act.wait_ge(cleared, 16 * (len(sums) + 1))

        @block.vector
        def _(dve):
            for n, s in enumerate("qk"):
                dve.wait_ge(wt_done, n + 1)
                if n:
                    dve.wait_ge(wf_done, n)
                for c in range(DC):
                    dve.tensor_copy(wT[:, c, :], pT[:, c, 0:D]).then_inc(wt_out, 1)
                dve.wait_ge(wf_done, n + 1)
                for c in range(DC):
                    dve.tensor_copy(wf[s][:, c, :], pQK[:, c, 0:D]).then_inc(wf_out, 1)
                dve.tensor_copy(bf[:, n, :], pQK[:, 2, 0:DC]).then_inc(wf_out, 1)
            dve.wait_ge(x_in, 64)
            dve.wait_ge(w_in, 96)
            dve.wait_ge(consts, 3)

            def norm(n):
                own = Chain(dve, dve_own, n * OWN_LN)
                rows = [tile_of(x_sb, v(n * GT) + j) for j in range(GT)]
                layer_norm_stats(dve, own, rows, stats, mom, var_ready)
                assert own.n == OWN_LN
                dve.wait_ge(rstd_ready, v(n + 1))
                if not early(n, 1):
                    dve.wait_ge(turned, v(n))
                for j in range(GT):
                    dve.tensor_scalar(xn[:, j, :], rows[j], mom[:, 4, j:j + 1], rstd[:, j:j + 1],
                                      ALU.subtract, ALU.mult).then_inc(xn_ready, 1)

            def group(n, s, turn, ahead):
                if ahead:
                    norm(n + 1)
                for j in range(4):
                    dve.wait_ge(part0_ready, v(n * 4 + (j + 1)))
                    dve.wait_ge(full_ready, v(n * 4 + (j + 1)))
                    if j >= 2 or not early(n, 1):
                        dve.wait_ge(parts_ready, v(n * 4 + (j - 1)))
                    dve.tensor_tensor(rest[:, j % 2, :], full[:, j % 2, :], parts[:, s, j, 0, :],
                                      ALU.subtract).then_inc(rest_ready, 1)
                    dve.wait_ge(rest_ready, v(n * 4 + (j + 1)))
                    dve.tensor_copy(parts[:, s, j, 1, :], rest[:, j % 2, :]).then_inc(part1_ready, 1)
                b = v(n) // QC
                for j in range(2):
                    dve.wait_ge(v_done, v(n * 2 + (j + 1)))
                    kt = (v(n) % QC) * GT + 2 * j
                    dst = v_sb[:, bass.ds(b, 1), :, bass.ds(kt, 2), :]
                    dve.tensor_tensor(dst.rearrange("p b h t d -> p (b h) t d"),
                                      pV[:, j, :].rearrange("p (t h d) -> p h t d", t=2, h=HEADS),
                                      bv[:, :].rearrange("p (h a d) -> p h a d", h=HEADS, a=1)
                                      .to_broadcast([P, HEADS, 2, DK]), ALU.add).then_inc(v_out, 1)

            OWN_LN = 10
            norm(0)
            turns(dve, group, GROUPS, 2, FIRST, LAST)
            dve.wait_ge(v_out, 2 * GROUPS)

        @block.tensor
        def _(pe):
            pe.wait_ge(consts, 5)
            pe.wait_ge(w_in, 96)
            pe.wait_ge(blocks, 16 * 2 * (P // DK))
            for n, s in enumerate("qk"):
                if n:
                    pe.wait_ge(wt_out, 2 * n)
                for c2 in range(DC):
                    for c in range(DC):
                        t = pe.transpose(pT[:, c2, c * P:(c + 1) * P], w_sb[s][:, c, c2 * P:(c2 + 1) * P], ident[:, :])
                t.then_inc(wt_done, 1)
                pe.wait_ge(wt_out, 2 * (n + 1))
                if n:
                    pe.wait_ge(wf_out, 3 * n)
                for c in range(DC):
                    for c2 in range(DC):
                        pe.matmul(pQK[:, c, c2 * P:(c2 + 1) * P], wT[:, c2, c * P:(c + 1) * P], wr[s][:, :],
                                  start=True, stop=True)
                for c2 in range(DC):
                    t = pe.matmul(pQK[:, 2, c2:c2 + 1], wr[s][:, :], bcol[s][:, c2:c2 + 1], start=True, stop=True)
                t.then_inc(wf_done, 1)
            pe.wait_ge(wf_out, 6)

            def turn_group(n):
                pe.wait_ge(xn_ready, v(n * GT + GT))
                if not early(n, 1):
                    pe.wait_ge(xnT_ready, v(n))
                for c in range(DC):
                    for j in range(GT):
                        t = pe.transpose(pT[:, c, j * P:(j + 1) * P], xn[:, j, c * P:(c + 1) * P], ident[:, :])
                t.then_inc(turned, 1)

            def group(n, s, turn, ahead):
                pe.wait_ge(xnT_ready, v(n + 1))
                for j in range(4):
                    side, c2 = "qk"[j // 2], j % 2
                    if not early(n, 1):
                        pe.wait_ge(part0_ready, v(n * 4 + (j - 3)))
                    for c in range(DC):
                        t = pe.matmul(pQK[:, j, :], wf[side][:, c, c2 * P:(c2 + 1) * P], xnT[:, s, c, :],
                                      start=(c == 0), stop=(c == DC - 1))
                    t.then_inc(qk_done, 1)
                if ahead:
                    turn_group(n + 1)
                for j in range(2):
                    if not early(n, 1):
                        pe.wait_ge(v_out, v(n * 2 + (j - 1)))
                    for q in range(2 * j, 2 * j + 2):
                        for c in range(DC):
                            t = pe.matmul(pV[:, j, (q % 2) * D:(q % 2 + 1) * D], xnT[:, s, c, q * P:(q + 1) * P],
                                          w_sb["v"][:, c, :], start=(c == 0), stop=(c == DC - 1))
                    t.then_inc(v_done, 1)
            turn_group(0)
            turns(pe, group, GROUPS, 2, FIRST, LAST)


def phase_attention(nc, v_sb, a_sb, q_dram, k_dram):
    SLOTS = 3
    NH = BATCH * HEADS
    STEPS = QC * KT
    HALF = 8
    GR = STEPS // HALF
    LEAD = KT
    LOADS = 2 * len(Q_PARTS)
    FIRST, LAST = 1, NH - 4
    assert (LAST - FIRST) % SLOTS == 0 and STEPS % SLOTS == 1
    with ExitStack() as ctx:
        m = Mem(nc, ctx, "att")
        qs = [m.sb(f"qs{s}", [ROWS, SEQ], BF16) for s in range(SLOTS)]
        ks = [m.sb(f"ks{s}", [ROWS, SEQ], BF16) for s in range(SLOTS)]
        vh = [m.sb(f"vh{s}", [P, KT, DK + 1]) for s in range(SLOTS)]
        probs = m.sb("probs", [P, 2 * HALF, GROUP])
        mx4 = [m.sb(f"mx4{s}", [P, KT, QC]) for s in range(SLOTS)]
        mx = m.sb("mx", [P, KT])
        nm = m.sb("nm", [P, SHIFT_ROWS, KT], BF16)
        nmT = m.sb("nmT", [SHIFT_ROWS * KT, P], BF16)
        identb = m.sb("identb", [P, P], BF16)
        comb = m.sb("comb", [P, QC, DK + 1])
        acc_sb = m.sb("acc_sb", [P, GROUP])
        rden = m.sb("rden", [P, QC, GT])

        pR = m.ps("pR", [P, 3, BANK])
        pS = m.ps("pS", [P, 3, BANK])
        pA = m.ps("pA", [P, BANK])
        pO = m.ps("pO", [P, BANK])
        O = pO[:, 0:KT * (DK + 1)].rearrange("p (t c d) -> p t c d", c=QC, d=DK + 1)
        NT = pO[0:SHIFT_ROWS * KT, 384:384 + P]

        qk_in = [m.sem(f"qk_in{s}") for s in range(SLOTS)]
        shift_in = [m.sem(f"shift_in{s}") for s in range(SLOTS)]
        consts = m.sem("consts")
        acc_clear = m.sem("acc_clear")
        v_in = m.sem("v_in")
        row_scored = m.sem("row_scored")
        maxed = m.sem("maxed")
        col_scored = m.sem("col_scored")
        expd = m.sem("expd")
        summed = m.sem("summed")
        acc_out = m.sem("acc_out")
        combined = m.sem("combined")
        mx_ready = m.sem("mx_ready")
        nm_hi = m.sem("nm_hi")
        nm_ready = m.sem("nm_ready")
        nm_turned = m.sem("nm_turned")
        nmT_ready = m.sem("nmT_ready")
        inverted = m.sem("inverted")
        normed = m.sem("normed")
        block = ctx.enter_context(nc.Block())

        def heads(eng, head, first=FIRST, last=LAST):
            for n in range(first):
                head(n, n % SLOTS, n // SLOTS, NH - 1 - n)
            with eng.Fori(0, (last - first) // SLOTS) as i:
                at = Step(eng, i)
                for n in range(first, first + SLOTS):
                    head(SLOTS * at + n, n % SLOTS, at + n // SLOTS, SLOTS)
            for n in range(last, NH):
                head(n, n % SLOTS, n // SLOTS, NH - 1 - n)

        def start(n):
            return isinstance(n, int) and n == 0

        @block.sync
        def _(sp):
            def load(n, s):
                for side, tile, sel in ((q_dram, qs[s], Q_PARTS), (k_dram, ks[s], K_PARTS)):
                    for r, part in enumerate(sel):
                        sp.dma_start(tile[DK * r:DK * r + DK, :],
                                     side[part, bass.ds(v(n * DK), DK), :]).then_inc(qk_in[s], 16)

            def shift(n, s):
                sp.wait_ge(nmT_ready, v(n + 1))
                for r in range(SHIFT_ROWS):
                    sp.dma_start(qs[s][PAIR_ROWS + r:PAIR_ROWS + r + 1, :].rearrange("a (t n) -> a t n", t=KT),
                                 nmT[KT * r:KT * r + KT, :]).then_inc(shift_in[s], 16)

            def head(n, s, turn, ahead):
                if ahead >= 2:
                    if not start(n):
                        sp.wait_ge(summed, v(GR * n - 1))
                    load(n + 2, (s + 2) % SLOTS)
                if ahead >= 1:
                    shift(n + 1, (s + 1) % SLOTS)

            load(0, 0)
            load(1, 1)
            shift(0, 0)
            heads(sp, head)

        @block.gpsimd
        def _(pool):
            make_identity(pool, identb[:, :], consts, 0)
            pool.memset(comb[:, :, :], 0.0).then_inc(consts, 1)
            for c in range(QC):
                pool.wait_ge(consts, 3 + c)
                pool.affine_select(out=comb[:, c, :], in_=comb[:, c, :], compare_op=ALU.not_equal, fill=1.0,
                                   base=-32 * c, pattern=[[-1, DK + 1]], channel_multiplier=1).then_inc(consts, 1)
            for s in range(SLOTS):
                pool.wait_ge(consts, 7 + 2 * s)
                pool.memset(ks[s][PAIR_ROWS:ROWS, :], 1.0).then_inc(consts, 1)
                pool.wait_ge(consts, 8 + 2 * s)
                pool.memset(vh[s][:, :, DK:DK + 1], 1.0).then_inc(consts, 1)
            pool.wait_ge(consts, 7 + 2 * SLOTS)

            def fetch(n, s):
                src = v_sb[:, :, :, :, :].rearrange("p b h t d -> p (b h) t d")[:, bass.ds(v(n), 1), :, :]
                pool.tensor_copy(vh[s][:, :, 0:DK], src.rearrange("p n t d -> p (n t) d")).then_inc(v_in, 1)

            def head(n, s, turn, ahead):
                if ahead >= 2:
                    if not start(n):
                        pool.wait_ge(summed, v(GR * n))
                    fetch(n + 2, (s + 2) % SLOTS)

            fetch(0, 0)
            fetch(1, 1)
            heads(pool, head)

        @block.scalar
        def _(act):
            def drain(n):
                act.wait_ge(summed, v(GR * n + GR))
                if not start(n):
                    act.wait_ge(combined, v(n))
                act.activation(acc_sb[:, :], pA[:, :], ACT.Copy).then_inc(acc_out, 1)

            def head(n, s, turn, ahead):
                for g in range(GR):
                    if not (start(n) and g < 2):
                        act.wait_ge(summed, v(GR * n + g - 1))
                    for j in range(HALF):
                        k = HALF * g + j
                        if j == 1 and g == 1 and not start(n):
                            drain(n - 1)
                        act.wait_ge(col_scored, v(STEPS * n + k + 1))
                        act.activation(probs[:, k % (2 * HALF), :], pS[:, (s + k) % 3, :], ACT.Exp,
                                       scale=float(DK) ** -0.5).then_inc(expd, 1)

            heads(act, head)
            drain(NH - 1)

        @block.vector
        def _(dve):
            dve.memset(pA[:, :], 0.0).then_inc(acc_clear, 1)

            def maxima(n, s, steps):
                for k in steps:
                    dve.wait_ge(row_scored, v(STEPS * n + k + 1))
                    dve.tensor_reduce(mx4[s][:, k // QC, k % QC:k % QC + 1], pR[:, (s + k) % 3, :],
                                      AX.X, ALU.max).then_inc(maxed, 1)

            def negate(n, s):
                dve.wait_ge(maxed, v(STEPS * n + STEPS))
                dve.tensor_reduce(mx[:, :], mx4[s][:, :, :], AX.X, ALU.max).then_inc(mx_ready, 1)
                dve.wait_ge(mx_ready, v(n + 1))
                dve.wait_ge(nm_turned, v(n))
                dve.tensor_scalar(nm[:, 0, :], mx[:, :], -1.0, None, ALU.mult).then_inc(nm_hi, 1)
                dve.wait_ge(nm_hi, v(n + 1))
                dve.scalar_tensor_tensor(out=nm[:, 1, :], in0=mx[:, :], scalar=-1.0, in1=nm[:, 0, :],
                                         op0=ALU.mult, op1=ALU.subtract).then_inc(nm_ready, 1)

            def send(n, s, turn_before, first=False):
                dve.wait_ge(nm_turned, v(n + 1))
                if not first:
                    dve.wait_ge(shift_in[(s + 2) % SLOTS], v(16 * SHIFT_ROWS * (turn_before + 1)))
                dve.tensor_copy(nmT[:, :], NT).then_inc(nmT_ready, 1)

            def normalise(n):
                dve.wait_ge(combined, v(n + 1))
                dve.reciprocal(rden[:, :, :], O[:, :, :, DK:DK + 1].rearrange("p t c a -> p c (t a)"))\
                   .then_inc(inverted, 1)
                dve.wait_ge(inverted, v(n + 1))
                dst = a_sb[:, :, :, :, :].rearrange("p b h t d -> p (b h) t d")[:, bass.ds(v(n), 1), :, :]
                dve.tensor_tensor(dst.rearrange("p n (c t) d -> p (n c) t d", c=QC),
                                  O[:, :, :, 0:DK].rearrange("p t c d -> p c t d"),
                                  rden[:, :, :].rearrange("p c (t a) -> p c t a", a=1).to_broadcast([P, QC, GT, DK]),
                                  ALU.mult).then_inc(normed, 1)

            def head(n, s, turn, ahead):
                s1, s2 = (s + 1) % SLOTS, (s + 2) % SLOTS
                if ahead >= 1:
                    maxima(n + 1, s1, range(LEAD, 2 * LEAD))
                if not start(n):
                    normalise(n - 1)
                if ahead >= 1:
                    maxima(n + 1, s1, range(2 * LEAD, STEPS))
                    negate(n + 1, s1)
                if ahead >= 2:
                    maxima(n + 2, s2, range(LEAD // 2))
                if ahead >= 1:
                    send(n + 1, s1, turn)
                if ahead >= 2:
                    maxima(n + 2, s2, range(LEAD // 2, LEAD))

            maxima(0, 0, range(STEPS))
            negate(0, 0)
            send(0, 0, 0, first=True)
            maxima(1, 1, range(LEAD))
            heads(dve, head)
            normalise(NH - 1)
            dve.wait_ge(normed, NH)

        @block.tensor
        def _(pe):
            pe.wait_ge(consts, 2 + 1 + 4 + 2 * SLOTS)
            pe.wait_ge(acc_clear, 1)

            def row_score(n, s, turn, k, first=False):
                if k == 0:
                    pe.wait_ge(qk_in[s], v(16 * LOADS * (turn + 1)))
                if not first:
                    pe.wait_ge(maxed, v(STEPS * n + k - 2))
                t, c = k // QC, k % QC
                pe.matmul(pR[:, (s + k) % 3, :], qs[s][0:PAIR_ROWS, t * P:(t + 1) * P],
                          ks[s][0:PAIR_ROWS, c * GROUP:(c + 1) * GROUP], start=True, stop=True).then_inc(row_scored, 1)

            def col_score(n, s, turn, k):
                if k == 0:
                    pe.wait_ge(shift_in[s], v(16 * SHIFT_ROWS * (turn + 1)))
                if not (start(n) and k < 3):
                    pe.wait_ge(expd, v(STEPS * n + k - 2))
                c, t = k % QC, k // QC
                pe.matmul(pS[:, (s + k) % 3, :], ks[s][:, t * P:(t + 1) * P],
                          qs[s][:, c * GROUP:(c + 1) * GROUP], start=True, stop=True).then_inc(col_scored, 1)

            def values(n, s, g, half):
                if half == 0:
                    pe.wait_ge(expd, v(STEPS * n + HALF * (g + 1)))
                    if g == 0:
                        pe.wait_ge(v_in, v(n + 1))
                        if not start(n):
                            pe.wait_ge(acc_out, v(n))
                for j in range(QC * half, QC * half + QC):
                    t, c = (HALF * g + j) // QC, j % QC
                    mm = pe.matmul(pA[32 * c:32 * c + DK + 1, :], vh[s][:, t, :],
                                   probs[:, (HALF * g + j) % (2 * HALF), :],
                                   start=(t == 0), stop=(t == KT - 1), skip_group_check=True)
                if half:
                    mm.then_inc(summed, 1)

            def combine(n, last=False):
                pe.wait_ge(acc_out, v(n + 1))
                if not start(n):
                    pe.wait_ge(normed, v(n))
                if not last:
                    pe.wait_ge(nmT_ready, v(n + 2))
                for t in range(GT):
                    mm = pe.matmul(O[:, t, :, :].rearrange("p c d -> p (c d)"), acc_sb[:, t * P:(t + 1) * P],
                                   comb[:, :, :].rearrange("p c d -> p (c d)"), start=True, stop=True)
                mm.then_inc(combined, 1)

            def turn_maxima(n, first=False):
                pe.wait_ge(nm_ready, v(n + 1))
                pe.wait_ge(nmT_ready, v(n))
                pe.matmul(NT, nm[:, :, :].rearrange("p r t -> p (r t)"), identb[:, :],
                          start=True, stop=True).then_inc(nm_turned, 1)

            def last_values(n, s, g, half):
                if g > 0:
                    values(n, s, g - 1, half)
                elif not start(n):
                    values(n - 1, (s + 2) % SLOTS, GR - 1, half)

            def head(n, s, turn, ahead):
                for g in range(GR):
                    for j in range(HALF):
                        k = HALF * g + j
                        col_score(n, s, turn, k)
                        over = (k + LEAD) // STEPS
                        if ahead >= 1 + over:
                            s_ahead = (s + 1 + over) % SLOTS
                            row_score(n + 1 + over, s_ahead, turn + (s + 1 + over) // SLOTS, (k + LEAD) % STEPS)
                        if j == 3:
                            last_values(n, s, g, 0)
                    if g == 1 and not start(n):
                        combine(n - 1)
                    last_values(n, s, g, 1)
                    if g == 6 and ahead >= 1:
                        turn_maxima(n + 1)

            for k in range(STEPS):
                row_score(0, 0, 0, k, first=(k < 3))
            turn_maxima(0)
            for k in range(LEAD):
                row_score(1, 1, 0, k)
            heads(pe, head)
            for half in range(2):
                values(NH - 1, (NH - 1) % SLOTS, GR - 1, half)
            combine(NH - 1, last=True)


def phase_attention_out(nc, io, x_sb, a_sb, ident):
    with ExitStack() as ctx:
        m = Mem(nc, ctx, "wo")
        wo = m.sb("wo", [P, DC, D])
        bo = m.sb("bo", [P, D])
        rows = m.sb("rows", [P, 2, GT, D])
        aT = m.sb("aT", [P, 2, DC, GROUP])
        pT = m.ps("pT", [P, DC, BANK])
        pO = m.ps("pO", [P, 2, BANK])
        w_in = m.sem("w_in")
        staged = m.sem("staged")
        turned = m.sem("turned")
        aT_ready = m.sem("aT_ready")
        made = m.sem("made")
        biased = m.sem("biased")
        added = m.sem("added")
        block = ctx.enter_context(nc.Block())

        @block.sync
        def _(sp):
            sp.dma_start(wo[:, :, :], io["WO"].rearrange("(c p) n -> p c n", p=P)).then_inc(w_in, 16)
            sp.dma_start(bo[:, :], row_bcast(io["bO"], D)).then_inc(w_in, 16)

        @block.gpsimd
        def _(pool):
            pool.wait_ge(w_in, 32)
            with pool.Fori(0, GROUPS) as g:
                rows_g = x_sb[:, bass.ds(g * GT, GT), :]
                pool.tensor_tensor(rows_g, rows_g,
                                   bo[:, :].rearrange("p (a n) -> p a n", a=1).to_broadcast([P, GT, D]),
                                   ALU.add).then_inc(biased, 1)

        @block.scalar
        def _(act):
            def stage(n, s):
                if not early(n, 2):
                    act.wait_ge(turned, v(n - 1))
                src = a_sb[:, bass.ds(v(n) // QC, 1), :, bass.ds((v(n) % QC) * GT, GT), :]
                act.activation(rows[:, s, :, :].rearrange("p t (h d) -> p h t d", d=DK),
                               src.rearrange("p b h t d -> p (b h) t d"), ACT.Copy).then_inc(staged, 1)

            def group(n, s, turn, ahead):
                act.wait_ge(turned, v(n + 1))
                if not early(n, 2):
                    act.wait_ge(made, v(n * 2 - 2))
                act.activation(aT[:, s, :, :], pT[:, :, :], ACT.Copy).then_inc(aT_ready, 1)
                if ahead >= 2:
                    stage(n + 2, s)
            stage(0, 0)
            stage(1, 1)
            turns(act, group, GROUPS, 2, 2, GROUPS - 2)

        @block.vector
        def _(dve):
            def group(n, s, turn, ahead):
                for j in range(2):
                    dve.wait_ge(made, v(n * 2 + (j + 1)))
                    dve.wait_ge(biased, v(n + 1))
                    pair = x_sb[:, bass.ds(v(n * GT) + 2 * j, 2), :]
                    dve.tensor_tensor(pair, pair, pO[:, j, :].rearrange("p (t d) -> p t d", t=2), ALU.add)\
                       .then_inc(added, 1)
            turns(dve, group, GROUPS, 2, 2, GROUPS - 2)
            dve.wait_ge(added, 2 * GROUPS)

        @block.tensor
        def _(pe):
            pe.wait_ge(w_in, 32)

            def turn_group(n, s):
                pe.wait_ge(staged, v(n + 1))
                if not early(n, 1):
                    pe.wait_ge(aT_ready, v(n))
                for c in range(DC):
                    for t in range(GT):
                        mm = pe.transpose(pT[:, c, t * P:(t + 1) * P], rows[:, s, t, c * P:(c + 1) * P], ident[:, :])
                mm.then_inc(turned, 1)

            def group(n, s, turn, ahead):
                if ahead:
                    turn_group(n + 1, (s + 1) % 2)
                pe.wait_ge(aT_ready, v(n + 1))
                for j in range(2):
                    if not early(n, 1):
                        pe.wait_ge(added, v(n * 2 + (j - 1)))
                    for t in range(2):
                        for c in range(DC):
                            at = (2 * j + t) * P
                            mm = pe.matmul(pO[:, j, t * D:(t + 1) * D], aT[:, s, c, at:at + P], wo[:, c, :],
                                           start=(c == 0), stop=(c == DC - 1))
                    mm.then_inc(made, 1)

            turn_group(0, 0)
            turns(pe, group, GROUPS, 2, 2, GROUPS - 2)


def phase_route(nc, io, tag, x_sb, ident, table, order, xnT_all):
    G = 4
    N = TILES // G
    HT = TILES // 2
    with ExitStack() as ctx:
        m = Mem(nc, ctx, tag)
        rw = m.sb("rw", [EXPERTS, D])
        rwT = m.sb("rwT", [P, DC, EXPERTS])
        ranki = m.sb("ranki", [P, TILES], I32)
        rank = m.sb("rank", [P, TILES])
        stats = m.sb("stats", [P, G, 6])
        mom = m.sb("mom", [P, 6, G])
        mhalf = m.sb("mhalf", [P, G])
        rstd = m.sb("rstd", [P, G])
        rows = m.sb("rows", [P, 2, G, ROW])
        xnT = m.sb("xnT", [P, DC, GROUP])
        lg = m.sb("lg", [P, G, EXPERTS])
        less = m.sb("less", [P, G, EXPERTS])
        mx = m.sb("mx", [P, G])
        left = m.sb("left", [P, G, EXPERTS])
        top = m.sb("top", [P, G, TOP])
        mask = m.sb("mask", [P, G, EXPERTS])
        ex = m.sb("ex", [P, G, EXPERTS])
        exm = m.sb("exm", [P, G, EXPERTS])
        den = m.sb("den", [P, G])
        rden = m.sb("rden", [P, G])
        val = m.sb("val", [P, 2, 2, EXPERTS])

        pT = m.ps("pT", [P, DC, BANK])
        pL = m.ps("pL", [P, 2, BANK])
        pV = m.ps("pV", [P, BANK])
        VT = pV[:, 0:2 * P]

        w_in = m.sem("w_in")
        consts = m.sem("consts")
        rw_turned = m.sem("rw_turned")
        rwT_ready = m.sem("rwT_ready")
        rank_ready = m.sem("rank_ready")
        dve_own = m.sem("dve_own")
        var_ready = m.sem("var_ready")
        rstd_ready = m.sem("rstd_ready")
        xn_ready = m.sem("xn_ready")
        turned = m.sem("turned")
        xnT_ready = m.sem("xnT_ready")
        logits = m.sem("logits")
        lg_out = m.sem("lg_out")
        lg_less = m.sem("lg_less")
        exp_ready = m.sem("exp_ready")
        weights = m.sem("weights")
        val_ready = m.sem("val_ready")
        val_turned = m.sem("val_turned")
        val_out = m.sem("val_out")
        kept = m.sem("kept")
        stored = [m.sem(f"stored{s}") for s in range(2)]
        block = ctx.enter_context(nc.Block())
        FIRST, LAST = 2, N - 2

        @block.sync
        def _(sp):
            sp.dma_start(rw[:, :], io["router_w"]).then_inc(w_in, 16)
            dst = table[0:TOK, :].rearrange("(h t p) c -> p h t c", p=P, h=2)

            def group(n, s, turn, ahead):
                sp.wait_ge(weights, v(n + 1))
                for h in range(2):
                    sp.dma_start(dst[:, h, bass.ds(v(n * 2), 2), :], rows[:, s, 2 * h:2 * h + 2, :])\
                      .then_inc(stored[s], 16)
            turns(sp, group, N, 2, FIRST, LAST)
            for s in range(2):
                sp.wait_ge(stored[s], 16 * 2 * N // 2)

        @block.gpsimd
        def _(pool):
            pool.memset(mhalf[:, :], -0.5).then_inc(consts, 1)
            pool.iota(ranki[:, :], [[-P, TILES]], base=TOK, channel_multiplier=-1).then_inc(consts, 1)

            def group(n, s, turn, ahead):
                pool.wait_ge(var_ready, v(n + 1))
                pool.tensor_tensor(rstd[:, :], mom[:, 5, :], mhalf[:, :], ALU.pow).then_inc(rstd_ready, 1)
            turns(pool, group, N, 2, FIRST, LAST)

        @block.scalar
        def _(act):
            def copy_xnT(n):
                act.wait_ge(turned, v(n + 1))
                if not early(n, 1):
                    act.wait_ge(logits, v(n))
                act.activation(xnT[:, :, :], pT[:, :, :], ACT.Copy).then_inc(xnT_ready, 1)
                act.activation(xnT_all[:, :, bass.ds(v(n * GROUP), GROUP)], pT[:, :, :], ACT.Copy).then_inc(kept, 1)

            def group(n, s, turn, ahead):
                if ahead:
                    copy_xnT(n + 1)
                act.wait_ge(lg_less, v(n + 1))
                if not early(n, 1):
                    act.wait_ge(weights, v(n))
                act.activation(ex[:, :, :], less[:, :, :], ACT.Exp).then_inc(exp_ready, 1)

            copy_xnT(0)
            turns(act, group, N, 2, FIRST, LAST)
            act.wait_ge(kept, N)

        @block.vector
        def _(dve):
            dve.wait_ge(consts, 2)
            dve.tensor_copy(rank[:, :], ranki[:, :]).then_inc(rank_ready, 1)
            dve.wait_ge(rw_turned, 1)
            dve.tensor_copy(rwT[:, :, :], pT[:, :, 0:EXPERTS]).then_inc(rwT_ready, 1)
            dve.wait_ge(rank_ready, 1)

            def moments(n):
                own = Chain(dve, dve_own, n * OWN_LN)
                layer_norm_stats(dve, own, [tile_of(x_sb, v(n * 2) + HT * (q // 2) + q % 2) for q in range(G)],
                                 stats, mom, var_ready)

            def norm(n, s, turn):
                dve.wait_ge(rstd_ready, v(n + 1))
                if not early(n, 2):
                    dve.wait_ge(stored[s], v(turn * 32))
                for q in range(G):
                    dve.tensor_scalar(rows[:, s, q, 0:D], tile_of(x_sb, v(n * 2) + HT * (q // 2) + q % 2),
                                      mom[:, 4, q:q + 1], rstd[:, q:q + 1],
                                      ALU.subtract, ALU.mult).then_inc(xn_ready, 1)

            OWN_LN = 10
            route_own = m.sem("route_own")
            OWN_ROUTE = 1 + 4 + 4 + 1 + 3

            def group(n, s, turn, ahead):
                if ahead:
                    moments(n + 1)
                if not early(n, 1):
                    keep_order(n - 1)
                if ahead:
                    norm(n + 1, (s + 1) % 2, turn + (s + 1) // 2)
                own = Chain(dve, route_own, n * OWN_ROUTE)
                dve.wait_ge(logits, v(n + 1))
                dve.tensor_copy(lg[:, :, :].rearrange("p g e -> p (g e)"), pL[:, s, 0:G * EXPERTS]).then_inc(lg_out, 1)
                dve.wait_ge(lg_out, v(n + 1))
                own(dve.tensor_reduce(mx[:, :], lg[:, :, :], AX.X, ALU.max))
                for q in range(G):
                    own(dve.max(top[:, q, :], lg[:, q, :]))
                own.settle()
                if not early(n, 1):
                    dve.wait_ge(exp_ready, v(n))
                dve.tensor_tensor(less[:, :, :], lg[:, :, :],
                                  mx[:, :].rearrange("p (g a) -> p g a", a=1).to_broadcast([P, G, EXPERTS]),
                                  ALU.subtract).then_inc(lg_less, 1)
                for q in range(G):
                    own(dve.match_replace(left[:, q, :], top[:, q, :], lg[:, q, :], NEG))
                own.settle()
                own(dve.tensor_tensor(mask[:, :, :], left[:, :, :], lg[:, :, :], ALU.not_equal))
                own.settle()
                if not early(n, 1):
                    dve.wait_ge(val_turned, v(n))
                rk = rank[:, :].rearrange("p (h t) -> p h t", h=2)[:, :, bass.ds(v(n * 2), 2)]
                dve.tensor_tensor(val[:, :, :, :].rearrange("p t h e -> p h t e"),
                                  mask[:, :, :].rearrange("p (h t) e -> p h t e", h=2),
                                  rk.rearrange("p h (t a) -> p h t a", a=1).to_broadcast([P, 2, 2, EXPERTS]),
                                  ALU.mult).then_inc(val_ready, 1)
                dve.wait_ge(exp_ready, v(n + 1))
                dve.wait_ge(val_ready, v(n + 1))
                own(dve.tensor_tensor(exm[:, :, :], ex[:, :, :], mask[:, :, :], ALU.mult))
                own.settle()
                own(dve.tensor_reduce(den[:, :], exm[:, :, :], AX.X, ALU.add))
                own.settle()
                own(dve.reciprocal(rden[:, :], den[:, :]))
                own.settle()
                assert own.n == OWN_ROUTE
                dve.tensor_tensor(rows[:, s, :, D:ROW], exm[:, :, :],
                                  rden[:, :].rearrange("p (g a) -> p g a", a=1).to_broadcast([P, G, EXPERTS]),
                                  ALU.mult).then_inc(weights, 1)

            def keep_order(n):
                dve.wait_ge(val_turned, v(n + 1))
                dve.tensor_copy(order[:, bass.ds(v(n * 256), 256)], VT).then_inc(val_out, 1)

            moments(0)
            norm(0, 0, 0)
            turns(dve, group, N, 2, FIRST, LAST)
            keep_order(N - 1)
            dve.wait_ge(val_out, N)
            dve.wait_ge(weights, N)

        @block.tensor
        def _(pe):
            pe.wait_ge(w_in, 16)
            for c in range(DC):
                mm = pe.transpose(pT[:, c, 0:EXPERTS], rw[:, c * P:(c + 1) * P], ident[0:EXPERTS, 0:EXPERTS])
            mm.then_inc(rw_turned, 1)
            pe.wait_ge(rwT_ready, 1)

            def turn_group(n, s):
                pe.wait_ge(xn_ready, v(n * 4 + 4))
                if not early(n, 1):
                    pe.wait_ge(kept, v(n))
                for c in range(DC):
                    for q in range(G):
                        mm = pe.transpose(pT[:, c, q * P:(q + 1) * P], rows[:, s, q, c * P:(c + 1) * P], ident[:, :])
                mm.then_inc(turned, 1)

            def logits_of(n, s):
                pe.wait_ge(xnT_ready, v(n + 1))
                if not early(n, 2):
                    pe.wait_ge(lg_out, v(n - 1))
                for q in range(G):
                    for c in range(DC):
                        mm = pe.matmul(pL[:, s, q * EXPERTS:(q + 1) * EXPERTS], xnT[:, c, q * P:(q + 1) * P],
                                       rwT[:, c, :], start=(c == 0), stop=(c == DC - 1))
                mm.then_inc(logits, 1)

            def group(n, s, turn, ahead):
                if ahead:
                    turn_group(n + 1, (s + 1) % 2)
                    logits_of(n + 1, (s + 1) % 2)
                pe.wait_ge(val_ready, v(n + 1))
                if not early(n, 1):
                    pe.wait_ge(val_out, v(n))
                for j in range(2):
                    mm = pe.transpose(VT[:, j * P:(j + 1) * P], val[:, j, :, :].rearrange("p h e -> p (h e)"),
                                      ident[:, :])
                mm.then_inc(val_turned, 1)

            turn_group(0, 0)
            logits_of(0, 0)
            turns(pe, group, N, 2, FIRST, LAST)


def phase_experts(nc, io, tag, x_sb, ident, order, xnT_all, table, sums):
    R = 6
    LEAD = 4
    HALF = 16 * R // 2
    G = 4
    N = TILES // G
    HT = TILES // 2
    with ExitStack() as ctx:
        m = Mem(nc, ctx, tag)
        firsts = m.sb("firsts", [P, CAP])
        both = m.sb("both", [EXPERTS, 2 * CAP])
        slots = m.sb("slots", [EXPERTS, CAP])
        sloti = m.sb("sloti", [P, 1], I32)
        slotf = m.sb("slotf", [P, 1])
        found = m.sb("found", [P, EXPERTS])
        empty = m.sb("empty", [P, EXPERTS])
        ids = m.sb("ids", [P, EXPERTS], I32)
        s_wgu = m.sb("s_wgu", [P, DC, 2 * FF])
        s_wd = m.sb("s_wd", [FP, FC, D])
        s_gu = m.sb("s_gu", [FP, 2, 2 * FC, GROUP])
        s_hh = m.sb("s_hh", [FP, 2, FC, GROUP])
        s_y = m.sb("s_y", [P, 2, 2 * D])
        wg = m.sb("wg", [P, R, DC, FF])
        wu = m.sb("wu", [P, R, DC, FF])
        wd = m.sb("wd", [FP, R, FC, D])
        idx = [m.sb(f"idx{s}", [P, 1], I32) for s in range(R)]
        xg = [m.sb(f"xg{s}", [P, ROW]) for s in range(R)]
        zero = m.sb("zero", [P, 1], I32)
        stood = m.sb("stood", [P, 2], I32)
        xT = m.sb("xT", [P, 2, DC * P])
        sg = m.sb("sg", [FP, 2, FC * P])
        hh = m.sb("hh", [FP, 2, FC * P])
        y = [m.sb(f"y{s}", [P, D]) for s in range(R)]
        pX = m.ps("pX", [P, 2, BANK])
        pG = m.ps("pG", [P, 2, BANK])
        pY = m.ps("pY", [P, 2, BANK])
        pI = m.ps("pI", [P, BANK])
        s_bank = [pX[0:FP, 0, :], pX[0:FP, 1, :], pG[0:FP, 0, :], pG[0:FP, 1, :]]

        ids_own = m.sem("ids_own")
        moved = m.sem("moved")
        listed = m.sem("listed")
        ids_turned = m.sem("ids_turned")
        ids_ready = m.sem("ids_ready")
        s_w_in = m.sem("s_w_in")
        s_gated = m.sem("s_gated")
        s_out = m.sem("s_out")
        s_hh_ready = m.sem("s_hh_ready")
        s_down = m.sem("s_down")
        s_y_ready = m.sem("s_y_ready")
        s_added = m.sem("s_added")
        w_in = [m.sem(f"w_in{s}") for s in range(R)]
        consts = m.sem("consts")
        stands = m.sem("stands")
        idx_ready = m.sem("idx_ready")
        x_in = [m.sem(f"x_in{s}") for s in range(R)]
        turned = m.sem("turned")
        xT_ready = m.sem("xT_ready")
        gated = m.sem("gated")
        silu_ready = m.sem("silu_ready")
        hh_ready = m.sem("hh_ready")
        down = m.sem("down")
        y_ready = m.sem("y_ready")
        summed = [m.sem(f"summed{s}") for s in range(2)]
        block = ctx.enter_context(nc.Block())
        FIRST = R + 1
        LAST = FIRST + (EXPERTS - FIRST - LEAD) // R * R

        @block.sync
        def _(sp):
            sp.dma_start(s_wgu[:, :, :], io["ws_gate_up"].rearrange("(c p) n -> p c n", p=P)).then_inc(s_w_in, 16)
            sp.dma_start(s_wd[:, :, :], io["ws_down"].rearrange("(c p) n -> p c n", p=FP)).then_inc(s_w_in, 16)

            def expert(n, s, turn, ahead):
                if isinstance(n, int) and n == R:
                    sp.wait_ge(listed, 1)
                    sp.dma_start(both[:, CAP:2 * CAP], firsts[EXPERTS:P, :]).then_inc(moved, 16)
                if not early(n, R):
                    sp.wait_ge(down, v(n - (R - 1)))
                for name, tile in (("w_gate", wg), ("w_up", wu)):
                    sp.dma_start(tile[:, s, :, :], io[name][bass.ds(v(n), 1), :, :]
                                 .rearrange("e (p c) f -> p (e c) f", c=DC)).then_inc(w_in[s], 16)
                sp.dma_start(wd[:, s, :, :], io["w_down"][bass.ds(v(n), 1), :, :]
                             .rearrange("e (p c) f -> p (e c) f", c=FC)).then_inc(w_in[s], 16)
            turns(sp, expert, EXPERTS, R, FIRST, LAST)

        @block.gpsimd
        def _(pool):
            pool.memset(zero[:, :], 0).then_inc(consts, 1)
            pool.iota(sloti[:, :], [[0, 1]], base=0, channel_multiplier=1).then_inc(consts, 1)
            pool.wait_ge(consts, 2)

            def shared_add(n):
                for h in range(2):
                    pool.wait_ge(s_y_ready, v(n * 2 + (h + 1)))
                    rows = x_sb[:, bass.ds(v(n * 2) + HT * h, 2), :]
                    pool.tensor_tensor(rows, rows, s_y[:, h, :].rearrange("p (t d) -> p t d", t=2), ALU.add)\
                        .then_inc(s_added, 1)

            def shared(n, s, turn, ahead):
                for c in range(FC):
                    pool.wait_ge(s_out, v(n * 4 + (c + 3)))
                    if not early(n, 2):
                        pool.wait_ge(s_down, v(n * 2 - 2))
                    pool.tensor_tensor(s_hh[:, s, c, :], s_gu[:, s, c, :], s_gu[:, s, FC + c, :], ALU.mult)\
                        .then_inc(s_hh_ready, 1)
                if not early(n, 1):
                    shared_add(n - 1)
            turns(pool, shared, N, 2, 2, N - 2)
            shared_add(N - 1)
            pool.wait_ge(ids_ready, 1)

            def stand(k):
                return pool.tensor_tensor(stood[:, k:k + 1], zero[:, :], zero[:, :], ALU.add)

            def gather(n, s, turn):
                pool.tensor_tensor(idx[s][:, :], ids[:, bass.ds(v(n), 1)], zero[:, :], ALU.add).then_inc(idx_ready, 1)
                pool.wait_ge(idx_ready, v(n + 1))
                if not early(n, R):
                    pool.wait_ge(y_ready, v(n - (R - 1)))
                stand(0)
                pool.indirect_dma_start(out=xg[s][:, :], out_offset=None, in_=table[:, :],
                                        in_offset=bass.IndirectOffsetOnAxis(ap=idx[s][:, 0:1], axis=0))\
                    .then_inc(x_in[s], 16)

            def expert(n, s, turn, ahead):
                if not early(n, 2):
                    pool.wait_ge(summed[s % 2], v(turn * HALF + 16 * (s // 2)))
                if ahead >= LEAD:
                    gather(n + LEAD, (s + LEAD) % R, turn + (s + LEAD) // R)
                pool.wait_ge(y_ready, v(n + 1))
                if not early(n, 1):
                    pool.wait_ge(stands, v(n))
                stand(1).then_inc(stands, 1)
                pool.indirect_dma_start(out=sums[s % 2][:, :],
                                        out_offset=bass.IndirectOffsetOnAxis(ap=idx[s][:, 0:1], axis=0),
                                        in_=y[s][:, :], in_offset=None, compute_op=ALU.add)\
                    .then_inc(summed[s % 2], 16)

            for n in range(LEAD):
                gather(n, n, 0)
            turns(pool, expert, EXPERTS, R, FIRST, LAST)
            pool.wait_ge(s_added, 2 * N)
            for q in range(2):
                pool.wait_ge(summed[q], 16 * EXPERTS // 2)

        @block.scalar
        def _(act):
            def shared_y(n, h):
                act.wait_ge(s_down, v(n * 2 + (h + 1)))
                if not early(n, 1):
                    act.wait_ge(s_added, v(n * 2 + (h - 1)))
                act.activation(s_y[:, h, :], pY[:, h, :], ACT.Copy).then_inc(s_y_ready, 1)

            def shared(n, s, turn, ahead):
                for f in range(2 * FC):
                    act.wait_ge(s_gated, v(n * 4 + (f + 1)))
                    if not early(n, 2):
                        act.wait_ge(s_hh_ready, v(n * 2 - 2))
                    act.activation(s_gu[:, s, f, :], s_bank[f], ACT.Silu if f < FC else ACT.Copy).then_inc(s_out, 1)
                    if f % 2 and not early(n, 1):
                        shared_y(n - 1, f // 2)
            turns(act, shared, N, 2, 2, N - 2)
            for h in range(2):
                shared_y(N - 1, h)

            def copy_x(n, q):
                act.wait_ge(turned, v(n + 1))
                if not early(n, 2):
                    act.wait_ge(gated, v(n - 1))
                act.activation(xT[:, q, :], pX[:, q, 0:DC * P], ACT.Copy).then_inc(xT_ready, 1)

            def expert(n, s, turn, ahead):
                if ahead:
                    copy_x(n + 1, (s + 1) % 2)
                act.wait_ge(gated, v(n + 1))
                if not early(n, 2):
                    act.wait_ge(hh_ready, v(n - 1))
                act.activation(sg[:, s % 2, :], pG[0:FP, s % 2, 0:FC * P], ACT.Silu).then_inc(silu_ready, 1)

            copy_x(0, 0)
            turns(act, expert, EXPERTS, R, FIRST, LAST)

        @block.vector
        def _(dve):
            own = Chain(dve, ids_own)

            def largest(out, src):
                for k in range(CAP // TOP):
                    own(dve.max(out[:, k * TOP:(k + 1) * TOP], src))
                    own.settle()
                    if k < CAP // TOP - 1:
                        own(dve.match_replace(src, out[:, k * TOP:(k + 1) * TOP], src, 0.0))
                        own.settle()

            largest(firsts, order[:, :])
            dve.tensor_copy(both[:, 0:CAP], firsts[0:EXPERTS, :]).then_inc(listed, 1)
            dve.wait_ge(listed, 1)
            dve.wait_ge(moved, 16)
            largest(slots, both[:, :])
            dve.wait_ge(consts, 2)
            dve.tensor_copy(slotf[:, :], sloti[:, :]).then_inc(listed, 1)
            dve.wait_ge(ids_turned, 1)
            dve.wait_ge(listed, 2)
            own(dve.tensor_scalar(found[:, :], pI[:, 0:EXPERTS], -1.0, float(TOK), ALU.mult, ALU.add))
            own(dve.tensor_scalar(empty[:, :], pI[:, 0:EXPERTS], 0.0, slotf[:, 0:1], ALU.is_equal, ALU.mult))
            own.settle()
            dve.tensor_tensor(ids[:, :], found[:, :], empty[:, :], ALU.add).then_inc(ids_ready, 1)

            def weigh(n, s, turn):
                dve.wait_ge(down, v(n + 1))
                if not early(n, R):
                    dve.wait_ge(summed[s % 2], v(turn * HALF + (16 * (s // 2 + 1) - HALF)))
                dve.tensor_scalar(y[s][:, :], pY[:, s % 2, 0:D], xg[s][:, bass.ds(v(n + D), 1)], None,
                                  ALU.mult).then_inc(y_ready, 1)

            def expert(n, s, turn, ahead):
                dve.wait_ge(silu_ready, v(n + 1))
                if not early(n, 2):
                    dve.wait_ge(down, v(n - 1))
                dve.tensor_tensor(hh[:, s % 2, :], sg[:, s % 2, :], pG[0:FP, s % 2, FC * P:2 * FC * P],
                                  ALU.mult).then_inc(hh_ready, 1)
                if not early(n, 1):
                    weigh(n - 1, (s - 1) % R, turn + (s - 1) // R)

            turns(dve, expert, EXPERTS, R, FIRST, LAST)
            weigh(EXPERTS - 1, (EXPERTS - 1) % R, (EXPERTS - 1) // R)

        @block.tensor
        def _(pe):
            pe.wait_ge(s_w_in, 32)

            def shared_down(n, s, h):
                pe.wait_ge(s_hh_ready, v(n * 2 + 2))
                if not early(n, 1):
                    pe.wait_ge(s_y_ready, v(n * 2 + (h - 1)))
                for q in range(2):
                    for c in range(FC):
                        at = (2 * h + q) * P
                        mm = pe.matmul(pY[:, h, q * D:(q + 1) * D], s_hh[:, s, c, at:at + P], s_wd[:, c, :],
                                       start=(c == 0), stop=(c == FC - 1))
                mm.then_inc(s_down, 1)

            def shared(n, s, turn, ahead):
                for f in range(2 * FC):
                    if not early(n, 1):
                        pe.wait_ge(s_out, v(n * 4 + (f - 3)))
                    for c in range(DC):
                        mm = pe.matmul(s_bank[f], s_wgu[:, c, f * FP:(f + 1) * FP],
                                       xnT_all[:, c, bass.ds(v(n * GROUP), GROUP)],
                                       start=(c == 0), stop=(c == DC - 1))
                    mm.then_inc(s_gated, 1)
                    if f % 2 and not early(n, 1):
                        shared_down(n - 1, (s + 1) % 2, f // 2)
            turns(pe, shared, N, 2, 2, N - 2)
            for h in range(2):
                shared_down(N - 1, (N - 1) % 2, h)
            pe.wait_ge(listed, 2)
            pe.transpose(pI[:, 0:EXPERTS], slots[:, :], ident[0:EXPERTS, 0:EXPERTS]).then_inc(ids_turned, 1)
            pe.wait_ge(s_out, 4 * N)
            pe.wait_ge(s_y_ready, 2 * N)

            def turn_x(n, s, turn):
                pe.wait_ge(x_in[s], v(turn * 16 + 16))
                if not early(n, 2):
                    pe.wait_ge(xT_ready, v(n - 1))
                cols = xg[s][:, 0:D].rearrange("t (p c) -> t c p", c=DC)
                for c in range(DC):
                    mm = pe.transpose(pX[:, s % 2, c * P:(c + 1) * P], cols[:, c, :], ident[:, :])
                mm.then_inc(turned, 1)

            def down_product(n, s):
                pe.wait_ge(hh_ready, v(n + 1))
                if not early(n, 2):
                    pe.wait_ge(y_ready, v(n - 1))
                for c in range(FC):
                    mm = pe.matmul(pY[:, s % 2, 0:D], hh[:, s % 2, c * P:(c + 1) * P], wd[:, s, c, :],
                                   start=(c == 0), stop=(c == FC - 1))
                mm.then_inc(down, 1)

            def expert(n, s, turn, ahead):
                if ahead:
                    turn_x(n + 1, (s + 1) % R, turn + (s + 1) // R)
                pe.wait_ge(xT_ready, v(n + 1))
                pe.wait_ge(w_in[s], v(turn * 48 + 48))
                if not early(n, 2):
                    pe.wait_ge(hh_ready, v(n - 1))
                for k, w in enumerate((wg, wu)):
                    cols = w[:, s, :, :].rearrange("p c (f k) -> p c k f", k=FC)
                    for f in range(FC):
                        for c in range(DC):
                            at = (FC * k + f) * P
                            mm = pe.matmul(pG[0:FP, s % 2, at:at + P], cols[:, c, f, :],
                                           xT[:, s % 2, c * P:(c + 1) * P], start=(c == 0), stop=(c == DC - 1))
                mm.then_inc(gated, 1)
                if not early(n, 1):
                    down_product(n - 1, (s - 1) % R)

            turn_x(0, 0, 0)
            turns(pe, expert, EXPERTS, R, FIRST, LAST)
            down_product(EXPERTS - 1, (EXPERTS - 1) % R)


def phase_merge(nc, tag, x_sb, sums, out):
    with ExitStack() as ctx:
        m = Mem(nc, ctx, tag)
        part = m.sb("part", [P, 2, 2, GT, D])
        s_in = [m.sem(f"s_in{s}") for s in range(2)]
        added = m.sem("added")
        stored = m.sem("stored")
        block = ctx.enter_context(nc.Block())
        FIRST, LAST = 2, GROUPS - 2

        def group_of(a, n):
            return a[:, bass.ds(v(n * GT), GT), :]

        @block.sync
        def _(sp):
            def load(n, s):
                if not early(n, 2):
                    sp.wait_ge(added, v((n - 1) * 2))
                for q in range(2):
                    src = sums[q][0:TOK, :].rearrange("(t p) d -> p t d", p=P)
                    sp.dma_start(part[:, s, q, :, :], group_of(src, n)).then_inc(s_in[s], 16)

            def group(n, s, turn, ahead):
                if ahead:
                    load(n + 1, (s + 1) % 2)
                sp.wait_ge(added, v(n * 2 + 2))
                dst = out.rearrange("b (t p) d -> p (b t) d", p=P)
                sp.dma_start(group_of(dst, n), group_of(x_sb, n)).then_inc(stored, 16)

            load(0, 0)
            turns(sp, group, GROUPS, 2, FIRST, LAST)
            sp.wait_ge(stored, 16 * GROUPS)

        @block.vector
        def _(dve):
            def group(n, s, turn, ahead):
                dve.wait_ge(s_in[s], v(turn * 32 + 32))
                for q in range(2):
                    if q:
                        dve.wait_ge(added, v(n * 2 + 1))
                    row = group_of(x_sb, n)
                    dve.tensor_tensor(row, row, part[:, s, q, :, :], ALU.add).then_inc(added, 1)
            turns(dve, group, GROUPS, 2, FIRST, LAST)
            dve.wait_ge(added, 2 * GROUPS)


def ffn(nc, io, tag, x_sb, ident, table, sums, out):
    with ExitStack() as ctx:
        m = Mem(nc, ctx, tag)
        order = m.sb("order", [P, TOK // 2])
        xnT_all = m.sb("xnT_all", [P, DC, TOK])
        phase_route(nc, io, tag + "r", x_sb, ident, table, order, xnT_all)
        phase_experts(nc, io, tag + "e", x_sb, ident, order, xnT_all, table, sums)
        if out is not None:
            phase_merge(nc, tag + "m", x_sb, sums, out)


STATES, DT_RANK = 16, 64
BC = 2 * STATES


def phase_ssm_in(nc, io, tag, x_sb, sums, ident, xnT, delta, du, bc3, negA, dcol, sel):
    with ExitStack() as ctx:
        m = Mem(nc, ctx, tag)
        wdt = m.sb("wdt", [P, DC, DT_RANK])
        wbc = m.sb("wbc", [P, DC, 3 * BC])
        wdp = m.sb("wdp", [DT_RANK, D])
        bcol = m.sb("bcol", [P, DC])
        alog = m.sb("alog", [P, DC, STATES])
        part = m.sb("part", [P, 2, 2, GT, D])
        stats = m.sb("stats", [P, GT, 6])
        mom = m.sb("mom", [P, 6, GT])
        mhalf = m.sb("mhalf", [P, GT])
        rstd = m.sb("rstd", [P, GT])
        xn = m.sb("xn", [P, GT, D])
        low = m.sb("low", [DT_RANK, GROUP])
        bc_hi = m.sb("bc_hi", [3 * BC, GROUP], BF16)
        bc_mid = m.sb("bc_mid", [3 * BC, GROUP], BF16)
        bc_rest = m.sb("bc_rest", [3 * BC, GROUP])
        size = m.sb("size", [P, DC, GROUP])
        pos = m.sb("pos", [P, DC, GROUP])
        e = m.sb("e", [P, DC, GROUP])
        ln = m.sb("ln", [P, DC, GROUP])
        e1 = m.sb("e1", [P, DC, GROUP])
        lost = m.sb("lost", [P, DC, GROUP])
        fixed = m.sb("fixed", [P, DC, GROUP])

        pT = m.ps("pT", [P, DC, BANK])
        pL = m.ps("pL", [P, BANK])
        pB = m.ps("pB", [P, BANK])
        pD = m.ps("pD", [P, DC, BANK])

        w_in = m.sem("w_in")
        a_ready = m.sem("a_ready")
        s_in = [m.sem(f"s_in{s}") for s in range(2)]
        merged = m.sem("merged")
        consts = m.sem("consts")
        dve_own = m.sem("dve_own")
        var_ready = m.sem("var_ready")
        rstd_ready = m.sem("rstd_ready")
        xn_ready = m.sem("xn_ready")
        turned = m.sem("turned")
        xnT_ready = m.sem("xnT_ready")
        projected = m.sem("projected")
        low_ready = m.sem("low_ready")
        hi_ready = m.sem("hi_ready")
        hi_placed = m.sem("hi_placed")
        bc_own = m.sem("bc_own")
        bc_ready = m.sem("bc_ready")
        dt_done = m.sem("dt_done")
        size_ready = m.sem("size_ready")
        pos_ready = m.sem("pos_ready")
        e_ready = m.sem("e_ready")
        ln_ready = m.sem("ln_ready")
        soft_own = m.sem("soft_own")
        delta_ready = m.sem("delta_ready")
        du_ready = m.sem("du_ready")
        block = ctx.enter_context(nc.Block())
        FIRST, LAST = 2, GROUPS - 2

        def cols(a, n):
            at = bass.ds(v(n * GROUP), GROUP)
            return a[:, :, at] if len(a.shape) == 3 else a[:, at]

        @block.sync
        def _(sp):
            def load(n, s):
                if not early(n, 2):
                    sp.wait_ge(merged, v(n * 2 - 2))
                for q in range(2):
                    src = sums[q][0:TOK, :].rearrange("(t p) d -> p t d", p=P)
                    sp.dma_start(part[:, s, q, :, :], src[:, bass.ds(v(n * GT), GT), :]).then_inc(s_in[s], 16)

            load(0, 0)
            sp.dma_start(wdt[:, :, :], io["W_dt"].rearrange("(c p) r -> p c r", p=P)).then_inc(w_in, 16)
            sp.dma_start(wdp[:, :], io["W_dtproj"]).then_inc(w_in, 16)
            with nc.allow_non_contiguous_dma(reason="short rows of small weights"):
                for r in range(3):
                    sp.dma_start(wbc[:, :, BC * r:BC * r + BC],
                                 io["W_bc"].rearrange("(c p) n -> p c n", p=P)).then_inc(w_in, 16)
                sp.dma_start(bcol[:, :], io["b_dtproj"].rearrange("(c p) -> p c", p=P)).then_inc(w_in, 16)
                sp.dma_start(dcol[:, :], io["D_param"].rearrange("(c p) -> p c", p=P)).then_inc(w_in, 16)
                sp.dma_start(alog[:, :, :], io["A_log"].rearrange("(c p) n -> p c n", p=P)).then_inc(w_in, 16)

            def group(n, s, turn, ahead):
                if ahead:
                    load(n + 1, (s + 1) % 2)
            turns(sp, group, GROUPS, 2, FIRST, LAST)

        @block.gpsimd
        def _(pool):
            pool.memset(mhalf[:, :], -0.5).then_inc(consts, 1)
            pool.memset(sel[:, :, :], 0.0).then_inc(consts, 1)
            for r in range(3):
                pool.wait_ge(consts, 2 + r)
                pool.affine_select(out=sel[:, :, :], in_=sel[:, :, :], compare_op=ALU.not_equal, fill=1.0,
                                   base=-BC * r, pattern=[[-1, BC], [0, P]], channel_multiplier=1)\
                    .then_inc(consts, 1)

            def merge(n, s, turn):
                pool.wait_ge(s_in[s], v(turn * 32 + 32))
                rows = x_sb[:, bass.ds(v(n * GT), GT), :]
                for q in range(2):
                    if q:
                        pool.wait_ge(merged, v(n * 2 + 1))
                    pool.tensor_tensor(rows, rows, part[:, s, q, :, :], ALU.add).then_inc(merged, 1)

            def product(n):
                pool.wait_ge(delta_ready, v(n + 1))
                pool.wait_ge(xnT_ready, v(n * 2 + 2))
                pool.tensor_tensor(cols(du, n), cols(delta, n), cols(xnT, n), ALU.mult).then_inc(du_ready, 1)

            def group(n, s, turn, ahead):
                pool.wait_ge(var_ready, v(n + 1))
                pool.tensor_tensor(rstd[:, :], mom[:, 5, :], mhalf[:, :], ALU.pow).then_inc(rstd_ready, 1)
                if ahead >= 2:
                    merge(n + 2, s, turn + 1)
                if not early(n, 1):
                    product(n - 1)
            merge(0, 0, 0)
            merge(1, 1, 0)
            turns(pool, group, GROUPS, 2, FIRST, LAST)
            product(GROUPS - 1)
            pool.wait_ge(du_ready, GROUPS)
            pool.wait_ge(consts, 5)

        @block.scalar
        def _(act):
            act.wait_ge(w_in, 16 * 8)
            act.activation(alog[:, :, :], alog[:, :, :], ACT.Exp).then_inc(a_ready, 1)

            def copy_xnT(n):
                act.wait_ge(turned, v(n + 1))
                act.activation(cols(xnT, n), pT[:, :, :], ACT.Copy).then_inc(xnT_ready, 2)

            def group(n, s, turn, ahead):
                act.wait_ge(projected, v(n * 2 + 1))
                if not early(n, 1):
                    act.wait_ge(dt_done, v(n))
                act.activation(low[:, :], pL[0:DT_RANK, :], ACT.Copy).then_inc(low_ready, 1)
                act.wait_ge(projected, v(n * 2 + 2))
                if not early(n, 1):
                    act.wait_ge(bc_ready, v(n * 2))
                act.activation(bc_hi[:, :], pB[0:3 * BC, :], ACT.Copy).then_inc(hi_ready, 1)
                act.wait_ge(hi_ready, v(n + 1))
                act.activation(cols(bc3, n)[0:BC, :], bc_hi[0:BC, :], ACT.Copy).then_inc(hi_placed, 1)
                act.wait_ge(dt_done, v(n + 1))
                if not early(n, 1):
                    act.wait_ge(e_ready, v(n))
                for c in range(DC):
                    act.activation(size[:, c, :], pD[:, c, :], ACT.Abs, bias=bcol[:, c:c + 1])\
                       .then_inc(size_ready, 1)
                act.wait_ge(size_ready, v(n * 2 + 2))
                if not early(n, 1):
                    act.wait_ge(delta_ready, v(n))
                act.activation(e[:, :, :], size[:, :, :], ACT.Exp, scale=-1.0).then_inc(e_ready, 1)
                if ahead:
                    copy_xnT(n + 1)
                act.wait_ge(e_ready, v(n + 1))
                act.activation(ln[:, :, :], e[:, :, :], ACT.Ln, bias=1.0).then_inc(ln_ready, 1)

            copy_xnT(0)
            turns(act, group, GROUPS, 2, FIRST, LAST)
            act.wait_ge(xnT_ready, 2 * GROUPS)
            act.wait_ge(hi_placed, GROUPS)

        @block.vector
        def _(dve):
            dve.wait_ge(a_ready, 1)
            dve.tensor_scalar(negA[:, :, :], alog[:, :, :], -1.0, None, ALU.mult).then_inc(a_ready, 1)
            dve.wait_ge(consts, 1)
            OWN_LN, OWN_BC, OWN_SOFT = 10, 2, 3

            def norm(n):
                own = Chain(dve, dve_own, n * OWN_LN)
                dve.wait_ge(merged, v(n * 2 + 2))
                layer_norm_stats(dve, own, [tile_of(x_sb, v(n * GT) + j) for j in range(GT)], stats, mom, var_ready)
                assert own.n == OWN_LN
                dve.wait_ge(rstd_ready, v(n + 1))
                if not early(n, 1):
                    dve.wait_ge(turned, v(n))
                for j in range(GT):
                    dve.tensor_scalar(xn[:, j, :], tile_of(x_sb, v(n * GT) + j), mom[:, 4, j:j + 1], rstd[:, j:j + 1],
                                      ALU.subtract, ALU.mult).then_inc(xn_ready, 1)

            def group(n, s, turn, ahead):
                if ahead:
                    norm(n + 1)
                own = Chain(dve, bc_own, n * OWN_BC)
                dve.wait_ge(hi_ready, v(n + 1))
                if not early(n, 1):
                    dve.wait_ge(bc_ready, v(n * 2))
                own(dve.tensor_tensor(bc_rest[:, :], pB[0:3 * BC, :], bc_hi[:, :], ALU.subtract))
                own.settle()
                own(dve.tensor_copy(bc_mid[:, :], bc_rest[:, :]))
                own.settle()
                dve.tensor_copy(cols(bc3, n)[BC:2 * BC, :], bc_mid[BC:2 * BC, :]).then_inc(bc_ready, 1)
                dve.tensor_tensor(cols(bc3, n)[2 * BC:3 * BC, :], bc_rest[2 * BC:3 * BC, :], bc_mid[2 * BC:3 * BC, :],
                                  ALU.subtract).then_inc(bc_ready, 1)
                dve.wait_ge(size_ready, v(n * 2 + 2))
                if not early(n, 1):
                    dve.wait_ge(delta_ready, v(n))
                for c in range(DC):
                    dve.tensor_scalar(pos[:, c, :], pD[:, c, :], bcol[:, c:c + 1], 0.0, ALU.add, ALU.max)\
                       .then_inc(pos_ready, 1)
                own = Chain(dve, soft_own, n * OWN_SOFT)
                dve.wait_ge(e_ready, v(n + 1))
                own(dve.tensor_scalar(e1[:, :, :], e[:, :, :], 1.0, -1.0, ALU.add, ALU.add))
                own.settle()
                own(dve.tensor_tensor(lost[:, :, :], e[:, :, :], e1[:, :, :], ALU.subtract))
                own.settle()
                dve.wait_ge(ln_ready, v(n + 1))
                own(dve.tensor_tensor(fixed[:, :, :], ln[:, :, :], lost[:, :, :], ALU.add))
                own.settle()
                dve.wait_ge(pos_ready, v(n * 2 + 2))
                dve.tensor_tensor(cols(delta, n), fixed[:, :, :], pos[:, :, :], ALU.add).then_inc(delta_ready, 1)

            norm(0)
            turns(dve, group, GROUPS, 2, FIRST, LAST)
            dve.wait_ge(delta_ready, GROUPS)
            dve.wait_ge(bc_ready, 2 * GROUPS)
            dve.wait_ge(a_ready, 2)

        @block.tensor
        def _(pe):
            pe.wait_ge(w_in, 16 * 8)

            def turn_group(n):
                pe.wait_ge(xn_ready, v(n * 4 + 4))
                if not early(n, 1):
                    pe.wait_ge(xnT_ready, v(n * 2))
                for c in range(DC):
                    for q in range(GT):
                        mm = pe.transpose(pT[:, c, q * P:(q + 1) * P], xn[:, q, c * P:(c + 1) * P], ident[:, :])
                mm.then_inc(turned, 1)

            def group(n, s, turn, ahead):
                pe.wait_ge(xnT_ready, v(n * 2 + 2))
                if not early(n, 1):
                    pe.wait_ge(low_ready, v(n))
                for c in range(DC):
                    mm = pe.matmul(pL[0:DT_RANK, :], wdt[:, c, :], cols(xnT, n)[:, c, :],
                                   start=(c == 0), stop=(c == DC - 1))
                mm.then_inc(projected, 1)
                if not early(n, 1):
                    pe.wait_ge(bc_ready, v(n * 2))
                for c in range(DC):
                    mm = pe.matmul(pB[0:3 * BC, :], wbc[:, c, :], cols(xnT, n)[:, c, :],
                                   start=(c == 0), stop=(c == DC - 1))
                mm.then_inc(projected, 1)
                pe.wait_ge(low_ready, v(n + 1))
                if not early(n, 1):
                    pe.wait_ge(pos_ready, v(n * 2))
                for c in range(DC):
                    mm = pe.matmul(pD[:, c, :], wdp[:, c * P:(c + 1) * P], low[:, :], start=True, stop=True)
                mm.then_inc(dt_done, 1)
                if ahead:
                    turn_group(n + 1)

            turn_group(0)
            turns(pe, group, GROUPS, 2, FIRST, LAST)


def phase_scan(nc, tag, ident, xnT, delta, du, bc3, negA, dcol, sel):
    SPAN = 2 * GROUP
    SPANS = SEQ // SPAN
    STEPS = SPANS * STATES
    KEPT = STEPS - STATES
    with ExitStack() as ctx:
        m = Mem(nc, ctx, tag)
        b_sb = [m.sb(f"b{s}", [P, SPAN]) for s in range(2)]
        decay = [m.sb(f"decay{s}", [P, SPAN]) for s in range(3)]
        bh = [m.sb(f"bh{s}", [P, DC, SPAN]) for s in range(3)]
        hc = [m.sb(f"hc{s}", [P, DC, SPAN]) for s in range(2)]
        carry = m.sb("carry", [P, DC, STATES])
        begun = m.sb("begun", [P, 8])
        pB = m.ps("pB", [P, 2, BANK])
        pC = m.ps("pC", [P, 2, BANK])
        pY = m.ps("pY", [P, DC, 2, BANK])

        consts = m.sem("consts")
        b_spread = m.sem("b_spread")
        c_spread = m.sem("c_spread")
        b_ready = m.sem("b_ready")
        decay_ready = m.sem("decay_ready")
        bx_ready = m.sem("bx_ready")
        h_ready = m.sem("h_ready")
        kept = m.sem("kept")
        hc_ready = m.sem("hc_ready")
        summed = m.sem("summed")
        y_ready = m.sem("y_ready")
        from_one = (b_ready, bx_ready, h_ready, kept, hc_ready, summed, y_ready)
        block = ctx.enter_context(nc.Block())

        def col(b, k):
            return bass.ds(b * SEQ + (k // STATES) * SPAN, SPAN)

        def begin(b, k, back=0):
            return b * STEPS + (max(k - back, 0) + 1)

        def begin2(b, k, back=0):
            return b * (2 * STEPS) + (2 * max(k - back, 0) + 1)

        @block.gpsimd
        def _(pool):
            for i, sem in enumerate(from_one):
                pool.memset(begun[:, i:i + 1], 0.0).then_inc(sem, 1)
            pool.memset(begun[:, 7:8], 0.0).then_inc(consts, 1)
            with pool.Fori(0, BATCH) as b:
                for k in range(STEPS):
                    s = k % 2
                    pool.wait_ge(b_ready, begin(b, k + 1))
                    pool.wait_ge(hc_ready, begin(b, k, 2))
                    if 3 <= k < KEPT + 3:
                        pool.wait_ge(kept, b * KEPT + (k - 1))
                    pool.tensor_tensor(bh[k % 3][:, :, :], du[:, :, col(b, k)],
                                       b_sb[s][:, :].rearrange("p (a n) -> p a n", a=1).to_broadcast([P, DC, SPAN]),
                                       ALU.mult).then_inc(bx_ready, 1)

        @block.scalar
        def _(act):
            act.wait_ge(consts, 1)

            def spread_b(b, k):
                act.wait_ge(b_spread, b * STEPS + k + 1)
                act.wait_ge(bx_ready, begin(b, k, 1))
                act.activation(b_sb[k % 2][:, :], pB[:, :, :].rearrange("p a n -> p (a n)"), ACT.Copy)\
                   .then_inc(b_ready, 1)

            def decays(b, k):
                n = k % STATES
                for c in range(DC):
                    i = DC * k + c
                    act.wait_ge(h_ready, b * (DC * STEPS) + (max(i - 2, 0) + 1))
                    act.activation(decay[i % 3][:, :], delta[:, c, col(b, k)], ACT.Exp,
                                   scale=negA[:, c, n:n + 1]).then_inc(decay_ready, 1)

            def keep(b, k):
                act.wait_ge(h_ready, begin2(b, k + 1))
                act.activation(carry[:, :, k % STATES:k % STATES + 1], bh[k % 3][:, :, SPAN - 1:SPAN],
                               ACT.Copy).then_inc(kept, 1)

            with act.Fori(0, BATCH) as b:
                spread_b(b, 0)
                decays(b, 0)
                spread_b(b, 1)
                for k in range(STEPS):
                    if 0 <= k - 1 < KEPT:
                        keep(b, k - 1)
                    if k + 1 < STEPS:
                        decays(b, k + 1)
                    if k + 2 < STEPS:
                        spread_b(b, k + 2)

        @block.vector
        def _(dve):
            dve.wait_ge(consts, 1)
            with dve.Fori(0, BATCH) as b:
                for k in range(STEPS):
                    s, n = k % 2, k % STATES
                    for c in range(DC):
                        dve.wait_ge(bx_ready, begin(b, k + 1))
                        dve.wait_ge(decay_ready, b * (2 * STEPS) + (2 * k + c + 1))
                        if k >= STATES:
                            dve.wait_ge(kept, b * KEPT + (k - STATES + 2))
                        dve.tensor_tensor_scan(bh[k % 3][:, c, :], decay[(DC * k + c) % 3][:, :], bh[k % 3][:, c, :],
                                               0.0 if k < STATES else carry[:, c, n:n + 1],
                                               ALU.mult, ALU.add).then_inc(h_ready, 1)
                    dve.wait_ge(h_ready, begin2(b, k + 1))
                    dve.wait_ge(c_spread, b * STEPS + k + 1)
                    dve.wait_ge(summed, begin(b, k, 1))
                    c_n = pC[:, :, :].rearrange("p a n -> p (a n)").rearrange("p (b n) -> p b n", b=1)
                    dve.tensor_tensor(hc[s][:, :, :], bh[k % 3][:, :, :], c_n.to_broadcast([P, DC, SPAN]),
                                      ALU.mult).then_inc(hc_ready, 1)
                    if n == STATES - 1:
                        dve.wait_ge(summed, begin(b, k + 1))
                        for c in range(DC):
                            x_c = xnT[:, c, col(b, k)]
                            dve.scalar_tensor_tensor(out=x_c, in0=x_c, scalar=dcol[:, c:c + 1],
                                                     in1=pY[:, c, :, :].rearrange("p a n -> p (a n)"),
                                                     op0=ALU.mult, op1=ALU.add).then_inc(y_ready, 1)
            dve.wait_ge(y_ready, BATCH * SPANS * DC + 1)

        @block.tensor
        def _(pe):
            pe.wait_ge(consts, 1)

            def spread(dst, row, b, k):
                for j in range(2):
                    at = bass.ds(b * SEQ + ((k // STATES) * SPAN + j * GROUP), GROUP)
                    mm = pe.matmul(dst[:, j, :], sel[:, row, :], bc3[:, at], start=True, stop=True)
                return mm

            def spread_b(b, k):
                pe.wait_ge(b_ready, begin(b, k))
                spread(pB, k % STATES, b, k).then_inc(b_spread, 1)

            def total(b, k, between=None):
                s, n = k % 2, k % STATES
                pe.wait_ge(hc_ready, begin(b, k + 1))
                if n == 0:
                    pe.wait_ge(y_ready, b * (SPANS * DC) + (DC * (k // STATES) + 1))
                for c in range(DC):
                    if c and between:
                        spread_b(*between)
                    for j in range(2):
                        mm = pe.matmul(pY[:, c, j, :], ident[:, :], hc[s][:, c, j * GROUP:(j + 1) * GROUP],
                                       start=(n == 0), stop=(n == STATES - 1))
                mm.then_inc(summed, 1)

            with pe.Fori(0, BATCH) as b:
                spread_b(b, 0)
                spread_b(b, 1)
                for k in range(STEPS):
                    pe.wait_ge(hc_ready, begin(b, k))
                    spread(pC, STATES + k % STATES, b, k).then_inc(c_spread, 1)
                    if k:
                        total(b, k - 1, (b, k + 2) if k + 2 < STEPS else None)
                    else:
                        spread_b(b, 2)
                total(b, STEPS - 1)


def phase_ssm_out(nc, tag, x_sb, yT, ident):
    with ExitStack() as ctx:
        m = Mem(nc, ctx, tag)
        y = m.sb("y", [P, 2, DC, 2 * P])
        pY = m.ps("pY", [P, 2, BANK])
        staged = m.sem("staged")
        turned = m.sem("turned")
        added = m.sem("added")
        block = ctx.enter_context(nc.Block())
        PAIRS = TILES // 2

        @block.scalar
        def _(act):
            def pair(n, s, turn, ahead):
                if not early(n, 2):
                    act.wait_ge(turned, v(n - 1))
                act.activation(y[:, s, :, :], yT[:, :, bass.ds(v(n * 2 * P), 2 * P)], ACT.Copy).then_inc(staged, 1)
            turns(act, pair, PAIRS, 2, 2, PAIRS - 2)

        @block.vector
        def _(dve):
            def pair(n, s, turn, ahead):
                dve.wait_ge(turned, v(n + 1))
                rows = x_sb[:, bass.ds(v(n * 2), 2), :]
                dve.tensor_tensor(rows, rows, pY[:, s, :].rearrange("p (t d) -> p t d", t=2), ALU.add)\
                   .then_inc(added, 1)
            turns(dve, pair, PAIRS, 2, 2, PAIRS - 2)
            dve.wait_ge(added, PAIRS)

        @block.tensor
        def _(pe):
            def pair(n, s, turn, ahead):
                pe.wait_ge(staged, v(n + 1))
                if not early(n, 2):
                    pe.wait_ge(added, v(n - 1))
                for t in range(2):
                    for c in range(DC):
                        mm = pe.transpose(pY[:, s, t * D + c * P:t * D + (c + 1) * P],
                                          y[:, s, c, t * P:(t + 1) * P], ident[:, :])
                mm.then_inc(turned, 1)
            turns(pe, pair, PAIRS, 2, 2, PAIRS - 2)


def state_space(nc, io, x_sb, sums, ident):
    with ExitStack() as ctx:
        m = Mem(nc, ctx, "ssm")
        xnT = m.sb("xnT", [P, DC, TOK])
        negA = m.sb("negA", [P, DC, STATES])
        dcol = m.sb("dcol", [P, DC])
        delta = m.sb("delta", [P, DC, TOK])
        du = m.sb("du", [P, DC, TOK])
        bc3 = m.sb("bc3", [3 * BC, TOK], BF16)
        sel = m.sb("sel", [3 * BC, BC, P], BF16)
        phase_ssm_in(nc, io, "si", x_sb, sums, ident, xnT, delta, du, bc3, negA, dcol, sel)
        phase_scan(nc, "sc", ident, xnT, delta, du, bc3, negA, dcol, sel)
        phase_ssm_out(nc, "so", x_sb, xnT, ident)


def build(nc, io, out):
    q_dram = nc.dram_tensor("query_parts", [3, BATCH * D, SEQ], BF16, kind="Internal").ap()
    k_dram = nc.dram_tensor("key_parts", [3, BATCH * D, SEQ], BF16, kind="Internal").ap()
    table = nc.dram_tensor("token_table", [TOK + P, ROW], F32, kind="Internal").ap()
    sums = [nc.dram_tensor(f"expert_sum{i}", [TOK + P, D], F32, kind="Internal").ap() for i in range(4)]
    nc.disable_value_cache = True
    with ExitStack() as ctx:
        m = Mem(nc, ctx, "all")
        ident = m.sb("ident", [P, P])
        x_sb = m.sb("x", [P, TILES, D])
        with ExitStack() as outputs:
            a_sb = Mem(nc, outputs, "all").sb("a", [P, BATCH, HEADS, KT, DK])
            with ExitStack() as values:
                v_sb = Mem(nc, values, "all").sb("v", [P, BATCH, HEADS, KT, DK])
                phase_qkv(nc, io, x_sb, v_sb, ident, q_dram, k_dram, sums, table)
                phase_attention(nc, v_sb, a_sb, q_dram, k_dram)
            phase_attention_out(nc, io, x_sb, a_sb, ident)
        ffn(nc, io, "f1", x_sb, ident, table, sums[0:2], None)
        state_space(nc, io, x_sb, sums[0:2], ident)
        ffn(nc, io, "f2", x_sb, ident, table, sums[2:4], out)


NAMES = {
    "L0_attn_a_": ("x", "WQ", "bQ", "WK", "bK", "WV", "bV", "WO", "bO", "WQr", "WKr"),
    "L0_attn_b_": ("A_log", "D_param", "W_bc", "W_dt", "W_dtproj", "b_dtproj"),
    "L0_ffn_": ("router_w", "w_gate", "w_up", "w_down", "ws_gate_up", "ws_down"),
}


def kernel(**inputs):
    import concourse.bacc as bacc
    from concourse.bass_utils import run_bass_kernel_spmd

    nc = bacc.Bacc("TRN2", target_bir_lowering=False, num_devices=1)
    arrays, io = {}, {}
    for prefix, names in NAMES.items():
        for name in names:
            a = np.ascontiguousarray(inputs[prefix + name])
            arrays[f"in_{name}"] = a
            io[name] = nc.dram_tensor(f"in_{name}", a.shape, mybir.dt.from_np(a.dtype), kind="ExternalInput").ap()
    out = nc.dram_tensor("out_x", (BATCH, SEQ, D), F32, kind="ExternalOutput").ap()
    build(nc, io, out)
    r = run_bass_kernel_spmd(nc, [arrays], core_ids=[0])
    return r.results[0]["out_x"]
```
